# Optimizing a Trainium2 kernel written in Bass

```python
import numpy as np
import jax
import jax.numpy as jnp

def _softmax(x, axis=-1):
    return jax.nn.softmax(x, axis=axis)

def _gelu(x):
    return jax.nn.gelu(x, approximate=True)

def _silu(x):
    return jax.nn.silu(x)

def _sigmoid(x):
    return jax.nn.sigmoid(x)

def _layernorm(x, axis=-1, eps=1e-05):
    m = jnp.mean(x, axis=axis, keepdims=True)
    v = jnp.var(x, axis=axis, keepdims=True)
    return (x - m) / jnp.sqrt(v + eps)

def _scatter_add(tgt, idx, src, axis=0):
    return tgt.at[idx].add(src)

def _segment_sum(src, seg, n):
    return jax.ops.segment_sum(src, seg, n)
kernel_name = 'mk_xattn_ffn_d2_seqx_r8_83f753'

def setup_inputs(seed: int=0):
    np.random.seed(seed)
    _w = jnp.asarray

    def _rec_inputs():
        import jax
        import jax.numpy as jnp
        _rk = jax.random.key(seed)
        x = -0.0003929 + 0.9999 * jax.random.normal(jax.random.fold_in(_rk, 1), (8, 128, 512), jnp.float32)
        _lenS = 128 - jax.random.randint(jax.random.fold_in(_rk, 7), (8,), 0, max(1, 128 // 4) + 1, jnp.int32)
        _lenS2 = 128 - jax.random.randint(jax.random.fold_in(_rk, 8), (8,), 0, max(1, 128 // 4) + 1, jnp.int32)
        _ctx_4096P = jax.random.normal(jax.random.fold_in(_rk, 11), (8, 16, 512), jnp.float32)
        _ctx_4096c = jax.random.dirichlet(jax.random.fold_in(_rk, 511), 0.3 * jnp.ones((16,), jnp.float32), (8, 128))
        _ctx_4096t = jnp.einsum('bsk,bkd->bsd', _ctx_4096c, _ctx_4096P)
        _ctx_4096t = _ctx_4096t * jax.lax.rsqrt(jnp.mean(jnp.square(_ctx_4096t)) + 1e-12) * 0.953939
        ctx_4096 = 2.81802e-05 + 1.00001 * (_ctx_4096t + 0.3 * jax.random.normal(jax.random.fold_in(_rk, 611), (8, 128, 512), jnp.float32))
        return (x, ctx_4096)
    x, ctx_4096 = _rec_inputs()

    def _L0_xattn_setup():
        import jax, jax.numpy as jnp
        import numpy as np
        EMBED = 512
        NUM_Q = 32
        NUM_KV = 8
        GROUPS = NUM_Q // NUM_KV
        HEAD_DIM = EMBED // NUM_Q
        KV_DIM = HEAD_DIM * NUM_KV
        key = jax.random.key(seed)
        ks = jax.random.split(key, 12)
        B, S = (2, 256)
        s = 0.02
        return {'query': jax.random.normal(ks[0], (B, S, EMBED), jnp.float32), 'key': jax.random.normal(ks[1], (B, S, EMBED), jnp.float32), 'value': jax.random.normal(ks[2], (B, S, EMBED), jnp.float32), 'Wq': jax.random.normal(ks[3], (EMBED, EMBED), jnp.float32) * s, 'bq': jnp.zeros((EMBED,), jnp.float32), 'Wk': jax.random.normal(ks[4], (EMBED, KV_DIM), jnp.float32) * s, 'bk': jnp.zeros((KV_DIM,), jnp.float32), 'Wv': jax.random.normal(ks[5], (EMBED, KV_DIM), jnp.float32) * s, 'bv': jnp.zeros((KV_DIM,), jnp.float32), 'Wo': jax.random.normal(ks[6], (EMBED, EMBED), jnp.float32) * s, 'bo': jnp.zeros((EMBED,), jnp.float32)}
    _L0_xattn_all = _L0_xattn_setup()
    _L0_xattn_in = {k: v for k, v in _L0_xattn_all.items() if k in ('Wq', 'bq', 'Wk', 'bk', 'Wv', 'bv', 'Wo', 'bo')}
    del _L0_xattn_all

    def _L0_ffn_setup():
        import jax, jax.numpy as jnp
        import numpy as np
        H = 512
        I = 256
        E = 16
        TOPK = 4
        SI = 256
        key = jax.random.key(seed)
        ks = jax.random.split(key, 9)
        s = 0.02
        return {'hidden_states': jax.random.normal(ks[0], (2, 256, H), dtype=jnp.float32), 'gate_w': jax.random.normal(ks[1], (E, H), dtype=jnp.float32) * s, 'bias': jnp.zeros((E,), dtype=jnp.float32), 'Wg': jax.random.normal(ks[2], (E, I, H), dtype=jnp.float32) * s, 'Wu': jax.random.normal(ks[3], (E, I, H), dtype=jnp.float32) * s, 'Wd': jax.random.normal(ks[4], (E, H, I), dtype=jnp.float32) * s, 'Sg': jax.random.normal(ks[5], (SI, H), dtype=jnp.float32) * s, 'Su': jax.random.normal(ks[6], (SI, H), dtype=jnp.float32) * s, 'Sd': jax.random.normal(ks[7], (H, SI), dtype=jnp.float32) * s}
    _L0_ffn_all = _L0_ffn_setup()
    _L0_ffn_in = {k: v for k, v in _L0_ffn_all.items() if k in ('gate_w', 'bias', 'Wg', 'Wu', 'Wd', 'Sg', 'Su', 'Sd')}
    del _L0_ffn_all

    def _L1_xattn_setup():
        import jax, jax.numpy as jnp
        import numpy as np
        import math
        HIDDEN = 512
        N_HEADS = 32
        HEAD_DIM = 128
        N_KV_HEADS = 4
        N_GROUPS = N_HEADS // N_KV_HEADS
        key = jax.random.key(seed)
        ks = jax.random.split(key, 6)
        B, NL, S = (8, 64, 512)
        latents = jax.random.normal(ks[0], (B, NL, HIDDEN), dtype=jnp.float32)
        context = jax.random.normal(ks[1], (B, S, HIDDEN), dtype=jnp.float32)
        scale = 1.0 / math.sqrt(HIDDEN)
        Wq = jax.random.normal(ks[2], (HIDDEN, N_HEADS * HEAD_DIM), dtype=jnp.float32) * scale
        Wk = jax.random.normal(ks[3], (HIDDEN, N_KV_HEADS * HEAD_DIM), dtype=jnp.float32) * scale
        Wv = jax.random.normal(ks[4], (HIDDEN, N_KV_HEADS * HEAD_DIM), dtype=jnp.float32) * scale
        Wo = jax.random.normal(ks[5], (N_HEADS * HEAD_DIM, HIDDEN), dtype=jnp.float32) * scale
        return {'latents': latents, 'context': context, 'Wq': Wq, 'Wk': Wk, 'Wv': Wv, 'Wo': Wo}
    _L1_xattn_all = _L1_xattn_setup()
    _L1_xattn_in = {k: v for k, v in _L1_xattn_all.items() if k in ('Wq', 'Wk', 'Wv', 'Wo')}
    del _L1_xattn_all

    def _L1_ffn_setup():
        import jax, jax.numpy as jnp
        import numpy as np
        B, S, IN, OUT = (4, 256, 512, 512)
        E, K, R = (8, 2, 16)
        CAP_FACTOR = 3.0
        ALPHA = 1.0 / R
        LN_EPS = 1e-05
        key = jax.random.key(seed)
        ks = jax.random.split(key, 6)
        return {'x': jax.random.normal(ks[0], (B, S, IN), dtype=jnp.float32), 'weight': jax.random.normal(ks[1], (OUT, IN), dtype=jnp.float32) * 0.02, 'lora_A': jax.random.normal(ks[2], (E, IN, R), dtype=jnp.float32) / np.sqrt(R), 'lora_B': jax.random.normal(ks[3], (E, R, OUT), dtype=jnp.float32) * 0.02, 'gw1': jax.random.normal(ks[4], (4 * E, IN), dtype=jnp.float32) * 0.02, 'gb1': jnp.zeros((4 * E,), dtype=jnp.float32), 'ln_gamma': jnp.ones((4 * E,), dtype=jnp.float32), 'ln_beta': jnp.zeros((4 * E,), dtype=jnp.float32), 'gw2': jax.random.normal(ks[5], (E, 4 * E), dtype=jnp.float32) * 0.02, 'gb2': jnp.zeros((E,), dtype=jnp.float32)}
    _L1_ffn_all = _L1_ffn_setup()
    _L1_ffn_in = {k: v for k, v in _L1_ffn_all.items() if k in ('weight', 'lora_A', 'lora_B', 'gw1', 'gb1', 'ln_gamma', 'ln_beta', 'gw2', 'gb2')}
    del _L1_ffn_all
    return {'x': x, 'ctx_4096': ctx_4096, 'L0_xattn_Wq': _L0_xattn_in['Wq'], 'L0_xattn_bq': _L0_xattn_in['bq'], 'L0_xattn_Wk': _L0_xattn_in['Wk'], 'L0_xattn_bk': _L0_xattn_in['bk'], 'L0_xattn_Wv': _L0_xattn_in['Wv'], 'L0_xattn_bv': _L0_xattn_in['bv'], 'L0_xattn_Wo': _L0_xattn_in['Wo'], 'L0_xattn_bo': _L0_xattn_in['bo'], 'L0_ffn_gate_w': _L0_ffn_in['gate_w'], 'L0_ffn_bias': _L0_ffn_in['bias'], 'L0_ffn_Wg': _L0_ffn_in['Wg'], 'L0_ffn_Wu': _L0_ffn_in['Wu'], 'L0_ffn_Wd': _L0_ffn_in['Wd'], 'L0_ffn_Sg': _L0_ffn_in['Sg'], 'L0_ffn_Su': _L0_ffn_in['Su'], 'L0_ffn_Sd': _L0_ffn_in['Sd'], 'L1_xattn_Wq': _L1_xattn_in['Wq'], 'L1_xattn_Wk': _L1_xattn_in['Wk'], 'L1_xattn_Wv': _L1_xattn_in['Wv'], 'L1_xattn_Wo': _L1_xattn_in['Wo'], 'L1_ffn_weight': _L1_ffn_in['weight'], 'L1_ffn_lora_A': _L1_ffn_in['lora_A'], 'L1_ffn_lora_B': _L1_ffn_in['lora_B'], 'L1_ffn_gw1': _L1_ffn_in['gw1'], 'L1_ffn_gb1': _L1_ffn_in['gb1'], 'L1_ffn_ln_gamma': _L1_ffn_in['ln_gamma'], 'L1_ffn_ln_beta': _L1_ffn_in['ln_beta'], 'L1_ffn_gw2': _L1_ffn_in['gw2'], 'L1_ffn_gb2': _L1_ffn_in['gb2']}

def reference(x, ctx_4096, L0_xattn_Wq, L0_xattn_bq, L0_xattn_Wk, L0_xattn_bk, L0_xattn_Wv, L0_xattn_bv, L0_xattn_Wo, L0_xattn_bo, L0_ffn_gate_w, L0_ffn_bias, L0_ffn_Wg, L0_ffn_Wu, L0_ffn_Wd, L0_ffn_Sg, L0_ffn_Su, L0_ffn_Sd, L1_xattn_Wq, L1_xattn_Wk, L1_xattn_Wv, L1_xattn_Wo, L1_ffn_weight, L1_ffn_lora_A, L1_ffn_lora_B, L1_ffn_gw1, L1_ffn_gb1, L1_ffn_ln_gamma, L1_ffn_ln_beta, L1_ffn_gw2, L1_ffn_gb2):
    import jax
    import jax.numpy as jnp

    def _L0_xattn_ref(query, key, value, Wq, bq, Wk, bk, Wv, bv, Wo, bo):
        import jax, jax.numpy as jnp
        import numpy as np
        EMBED = 512
        NUM_Q = 32
        NUM_KV = 8
        GROUPS = NUM_Q // NUM_KV
        HEAD_DIM = EMBED // NUM_Q
        KV_DIM = HEAD_DIM * NUM_KV
        B, S, _ = query.shape
        Q = query @ Wq + bq
        K = key @ Wk + bk
        V = value @ Wv + bv
        Q = Q.reshape(B, S, NUM_KV, GROUPS, HEAD_DIM).transpose(0, 2, 3, 1, 4)
        K = K.reshape(B, S, NUM_KV, HEAD_DIM).transpose(0, 2, 1, 3)
        V = V.reshape(B, S, NUM_KV, HEAD_DIM).transpose(0, 2, 1, 3)
        scale = 1.0 / jnp.sqrt(jnp.asarray(HEAD_DIM, query.dtype))
        scores = jnp.einsum('bhgqd,bhkd->bhgqk', Q, K) * scale
        w = jax.nn.softmax(scores, axis=-1)
        y = jnp.einsum('bhgqk,bhkd->bhgqd', w, V)
        y = y.transpose(0, 3, 1, 2, 4).reshape(B, S, EMBED)
        return y @ Wo + bo

    def _L0_ffn_ref(hidden_states, gate_w, bias, Wg, Wu, Wd, Sg, Su, Sd):
        import jax, jax.numpy as jnp
        import numpy as np
        H = 512
        I = 256
        E = 16
        TOPK = 4
        SI = 256
        orig_shape = hidden_states.shape
        x = hidden_states.reshape(-1, orig_shape[-1])
        scores = jax.nn.sigmoid(x @ gate_w.T) + bias
        topk_w, topk_idx = jax.lax.top_k(scores, TOPK)
        topk_w = topk_w / (jnp.sum(topk_w, axis=-1, keepdims=True) + 1e-20)
        cw = jnp.sum(jax.nn.one_hot(topk_idx, E, dtype=x.dtype) * topk_w[..., None], axis=1)
        g = jnp.einsum('th,eih->eti', x, Wg)
        u = jnp.einsum('th,eih->eti', x, Wu)
        z = jax.nn.silu(g) * u
        zw = z * cw.T[:, :, None]
        out = jnp.einsum('eti,ehi->th', zw, Wd)
        out = out + jax.nn.silu(x @ Sg.T) * (x @ Su.T) @ Sd.T
        return out.reshape(orig_shape)

    def _L1_xattn_ref(latents, context, Wq, Wk, Wv, Wo):
        import jax, jax.numpy as jnp
        import numpy as np
        import math
        HIDDEN = 512
        N_HEADS = 32
        HEAD_DIM = 128
        N_KV_HEADS = 4
        N_GROUPS = N_HEADS // N_KV_HEADS
        b, q_len, _ = latents.shape
        kv_len = q_len + context.shape[1]
        hidden_states = jnp.concatenate([context, latents], axis=1)
        q = (latents @ Wq).reshape(b, q_len, N_KV_HEADS, N_GROUPS, HEAD_DIM)
        k = (hidden_states @ Wk).reshape(b, kv_len, N_KV_HEADS, HEAD_DIM)
        v = (hidden_states @ Wv).reshape(b, kv_len, N_KV_HEADS, HEAD_DIM)
        scale = 1.0 / math.sqrt(HEAD_DIM)
        scores = jnp.einsum('bqhgd,bkhd->bhgqk', q, k) * scale
        attn = jax.nn.softmax(scores.astype(jnp.float32), axis=-1).astype(q.dtype)
        out = jnp.einsum('bhgqk,bkhd->bqhgd', attn, v)
        out = out.reshape(b, q_len, N_HEADS * HEAD_DIM)
        return out @ Wo

    def _L1_ffn_ref(x, weight, lora_A, lora_B, gw1, gb1, ln_gamma, ln_beta, gw2, gb2):
        import jax, jax.numpy as jnp
        import numpy as np
        B, S, IN, OUT = (4, 256, 512, 512)
        E, K, R = (8, 2, 16)
        CAP_FACTOR = 3.0
        ALPHA = 1.0 / R
        LN_EPS = 1e-05
        orig_shape = x.shape
        xf = x.reshape(-1, orig_shape[-1])
        N = xf.shape[0]
        capacity = int(CAP_FACTOR * N / E)
        h = xf @ gw1.T + gb1
        mu = jnp.mean(h, axis=-1, keepdims=True)
        var = jnp.mean((h - mu) ** 2, axis=-1, keepdims=True)
        h = (h - mu) * jax.lax.rsqrt(var + LN_EPS) * ln_gamma + ln_beta
        h = jax.nn.relu(h)
        gates = h @ gw2.T + gb2
        top_v, top_i = jax.lax.top_k(gates, K)
        top_g = jax.nn.softmax(top_v, axis=-1)
        onehot = (top_i[..., None] == jnp.arange(E)).astype(xf.dtype)
        counts = onehot.sum(axis=0)
        allowed = (counts <= capacity).astype(xf.dtype)
        w = jnp.einsum('nke,nk,ke->ne', onehot, top_g, allowed)
        main = xf @ weight.T
        tmp = jnp.einsum('ni,eir->enr', xf, lora_A)
        tmp = tmp * w.T[:, :, None]
        lora = jnp.einsum('enr,ero->no', tmp, lora_B) * ALPHA
        out = main + lora
        return out.reshape(*orig_shape[:-1], weight.shape[0])
    x = x + _L0_xattn_ref(_layernorm(x, axis=-1), ctx_4096, ctx_4096, L0_xattn_Wq, L0_xattn_bq, L0_xattn_Wk, L0_xattn_bk, L0_xattn_Wv, L0_xattn_bv, L0_xattn_Wo, L0_xattn_bo)
    x = x + _L0_ffn_ref(_layernorm(x, axis=-1), L0_ffn_gate_w, L0_ffn_bias, L0_ffn_Wg, L0_ffn_Wu, L0_ffn_Wd, L0_ffn_Sg, L0_ffn_Su, L0_ffn_Sd)
    x = x + _L1_xattn_ref(_layernorm(x, axis=-1), ctx_4096, L1_xattn_Wq, L1_xattn_Wk, L1_xattn_Wv, L1_xattn_Wo)
    x = x + _L1_ffn_ref(_layernorm(x, axis=-1), L1_ffn_weight, L1_ffn_lora_A, L1_ffn_lora_B, L1_ffn_gw1, L1_ffn_gb1, L1_ffn_ln_gamma, L1_ffn_ln_beta, L1_ffn_gw2, L1_ffn_gb2)
    return x

_drawn_inputs = setup_inputs


def setup_inputs(seed=0):
    import zlib

    import numpy as np

    out = dict(_drawn_inputs(seed))
    spreads = {'L0_xattn_bq': (0.0, 0.8),
     'L0_xattn_bk': (0.0, 0.8),
     'L0_xattn_bv': (0.0, 0.1),
     'L0_xattn_bo': (0.0, 0.1),
     'L0_ffn_bias': (0.0, 0.6),
     'L1_ffn_gb1': (0.0, 0.8),
     'L1_ffn_ln_gamma': (1.0, 0.6),
     'L1_ffn_ln_beta': (0.0, 0.8),
     'L1_ffn_gb2': (0.0, 0.648)}
    factors = {'L0_xattn_Wq': 8.0,
     'L0_xattn_Wk': 7.515,
     'L0_ffn_gate_w': 5.037,
     'L0_ffn_Wg': 3.841,
     'L0_ffn_Wu': 3.778,
     'L0_ffn_Wd': 3.754,
     'L1_ffn_lora_A': 6.209,
     'L1_ffn_lora_B': 6.198,
     'L1_ffn_gw1': 6.954,
     'L1_ffn_gw2': 6.584}
    for name, (base, spread) in spreads.items():
        noise = np.random.default_rng([zlib.crc32(name.encode()), seed]).standard_normal(out[name].shape)
        drawn = base * np.exp(spread * noise) if base else spread * noise
        out[name] = jnp.asarray(drawn.astype(out[name].dtype))
    for name, factor in factors.items():
        out[name] = (out[name] * factor).astype(out[name].dtype)
    return out
```

```python
from contextlib import ExitStack

import concourse.bass as bass
from concourse import mybir

F32 = mybir.dt.float32
F32R = mybir.dt.float32r
U32 = mybir.dt.uint32
ALU = mybir.AluOpType
ACT = mybir.ActivationFunctionType
AX = mybir.AxisListType

P = 128
B = 8
D = 512
KT = D // P
HB = B // 2
HT = HB * P
LN_EPS = 1e-5

H0, KV0, HD0 = 32, 8, 16
G0 = H0 // KV0
E0, TOP0, I0 = 16, 4, 256
IT = I0 // P
H1, KV1 = 32, 4
UH = 4
UNITS = H1 // UH
SCALE0 = 0.25
SCALE1 = float(P) ** -0.5
E1, TOP1, R1 = 8, 2, 16
G1 = 4 * E1
SMALL = P + G1
CAPACITY = int(3.0 * B * P / E1)

C_ID, C_SEL, C_ONES, C_MASK, C_IOTA, C_EPS = 0, 128, 640, 768, 770, 786
CONST = 787


class Queue:

    def __init__(self, eng, sem):
        self.eng, self.sem, self.count, self.seen = eng, sem, 0, {}

    def wait(self, *tokens):
        for t in tokens:
            if t is None:
                continue
            sem, value = t
            if self.seen.get(sem.name, 0) < value:
                self.eng.wait_ge(sem, value)
                self.seen[sem.name] = value

    def did(self, ins):
        self.count += 1
        ins.then_inc(self.sem, 1)
        return (self.sem, self.count)

    def last(self):
        return (self.sem, self.count)


class Ring:

    def __init__(self, bufs):
        self.bufs, self.reader, self.at = bufs, [None] * len(bufs), 0

    def take(self):
        i = self.at % len(self.bufs)
        self.at += 1
        return i, self.bufs[i], self.reader[i]

    def release(self, i, token):
        self.reader[i] = token


class Landing(Ring):

    def __init__(self, bufs, sems):
        super().__init__(bufs)
        self.sems, self.fills = sems, [0] * len(bufs)

    def filled(self, i, ins):
        self.fills[i] += 1
        ins.then_inc(self.sems[i], 16)
        return (self.sems[i], 16 * self.fills[i])


def three(hi_lo_a, hi_lo_b):
    (ah, al), (bh, bl) = hi_lo_a, hi_lo_b
    return (ah, bh), (ah, bl), (al, bh)


def layers_kernel(nc, A, out):
    with ExitStack() as whole:
        scope = [whole]

        def sb(name, shape, dt=F32):
            return scope[-1].enter_context(nc.sbuf_tensor(name, shape, dt))

        def pair(name, shape):
            return sb(name + "_hi", shape, F32R), sb(name + "_lo", shape, F32R)

        def sem(name):
            return whole.enter_context(nc.semaphore(name))

        pe = Queue(nc.tensor, sem("pe_done"))
        act = Queue(nc.scalar, sem("act_done"))
        dve = Queue(nc.vector, sem("dve_done"))
        pool = Queue(nc.gpsimd, sem("pool_done"))
        sp = Queue(nc.sync, sem("sp_unused"))

        def load(dst, src, sem_):
            nc.sync.dma_start(dst, src).then_inc(sem_, 16)
            return (sem_, 16)

        def loaded(name, dst, src):
            return load(dst, src, sem("ld_" + name))

        def split(hi, lo, src, ready, free=None, hi_on=None):
            if hi_on is pool:
                pool.wait(*ready, free)
                t = pool.did(nc.gpsimd.tensor_copy(hi, src))
            else:
                act.wait(*ready, free)
                t = act.did(nc.scalar.activation(hi, src, ACT.Copy))
            dve.wait(t, *ready, free)
            return dve.did(nc.vector.tensor_tensor(lo, src, hi.bitcast(F32), ALU.subtract))

        def mm_group(dst, pairs, mark=True):
            pairs = list(pairs)
            for n, (a, b) in enumerate(pairs):
                ins = nc.tensor.matmul(dst, a, b, start=(n == 0), stop=(n == len(pairs) - 1))
            return pe.did(ins) if mark else None

        def fence():
            tokens = [q.last() for q in (pe, act, dve, pool) if q.count]
            for q in (pe, act, dve, pool, sp):
                q.wait(*tokens)

        bank = [whole.enter_context(nc.psum_tensor(f"bank{i}", [P, 512], F32)) for i in range(8)]

        x = sb("x", [P, B, D])
        x_ready = [None] * B
        xnA = pair("xnA", [P, KT, HT])
        consts = sb("consts", [P, CONST])
        ident = consts[:, C_ID:C_ID + P]
        ones = consts[:, C_ONES:C_ONES + P]
        eps = consts[:, C_EPS:C_EPS + 1]
        iota = consts[:, C_IOTA:C_IOTA + 16]
        stats = sb("stats", [P, B, 6])
        moments = sb("moments", [P, B, 2])
        rstd = sb("rstd", [P, B])
        xn = [sb(f"xn{i}", [P, D]) for i in range(2)]
        xn_ring = Ring(xn)

        t_const = loaded("consts", consts[:, :], A["consts"])
        s_x = [sem(f"ld_x{b}") for b in range(B)]

        def layer_norm(tiles, dest, banks, dest_free=None):
            b0 = tiles[0]
            for b in tiles:
                dve.wait(x_ready[b])
                t = dve.did(nc.vector.bn_stats(stats[:, b, :], x[:, b, :]))
                dve.wait(t)
                t = dve.did(nc.vector.bn_aggr(moments[:, b, :], stats[:, b, :]))
            act.wait(t, t_const)
            r = rstd[:, b0:b0 + len(tiles)]
            t = act.did(nc.scalar.activation(r, moments[:, b0:b0 + len(tiles), 1], ACT.Sqrt, bias=eps))
            dve.wait(t)
            t_r = dve.did(nc.vector.reciprocal(r, r))
            for n, b in enumerate(tiles):
                i, buf, free = xn_ring.take()
                dve.wait(t_r, free)
                t = dve.did(nc.vector.tensor_scalar(buf[:, :], x[:, b, :], moments[:, b, 0:1],
                                                    rstd[:, b:b + 1], ALU.subtract, ALU.mult))
                j, ps, ps_free = banks.take()
                pe.wait(t, t_const, ps_free)
                for k in range(KT):
                    ins = nc.tensor.transpose(ps[:, k * P:(k + 1) * P], buf[:, k * P:(k + 1) * P], ident)
                t = pe.did(ins)
                xn_ring.release(i, t)
                cols = slice((b % HB) * P, (b % HB + 1) * P)
                ps3 = ps[:, :].rearrange("p (k t) -> p k t", k=KT)
                t = split(dest[0][:, :, cols], dest[1][:, :, cols], ps3, [t], dest_free)
                banks.release(j, t)
            return t

        with ExitStack() as phase:
            scope.append(phase)
            ctxT = pair("ctx0", [P, KT, HT])
            w_raw = sb("w0_raw", [P, KT, D])
            wq = pair("wq0", [P, KT, D])
            wkv = pair("wkv0", [P, 2, KT, P])
            wo = pair("wo0", [P, KT, D])
            sel = sb("sel", [P, KT, P], F32R)
            qT = pair("q0T", [P, KT, HT])
            kT = pair("k0T", [P, HT])
            kd = pair("k0d", [P, KT, 2, HT])
            v = sb("v0", [P, HB, P])
            vp = [pair(f"v0p{i}", [P, KV0, P]) for i in range(2)]
            bq = sb("bq0", [P, KT])
            bk = sb("bk0", [P, 1])
            bv = sb("bv0", [P, P])
            bo = sb("bo0", [P, D])
            pr = [sb(f"p0_{i}", [P, 16, P]) for i in range(2)]
            pT = [pair(f"p0T{i}", [P, HT]) for i in range(2)]
            aT = pair("a0T", [P, G0 * P])
            mx = [sb(f"mx0_{i}", [P, 16]) for i in range(2)]
            nb = [sb(f"nb0_{i}", [P, 16]) for i in range(2)]
            sm = [sb(f"sm0_{i}", [P, 16]) for i in range(2)]
            ri = [sb(f"ri0_{i}", [P, 16]) for i in range(2)]

            ctxT_raw = pr[1][:, :, :].rearrange("p a c -> p (a c)").rearrange("p (k t) -> p k t", k=KT)
            small_raw = pr[0][:, 0:2 * KT, :].rearrange("p (n k) c -> p n k c", n=2)
            mask = consts[:, C_MASK:C_MASK + 2]
            s_ctx = sem("ld_ctx0")

            for b in range(HB):
                x_ready[b] = load(x[:, b, :], A["x"][b], s_x[b])
            t_wq = loaded("wq0", w_raw[:, :, :], A["wq0"])
            nc.sync.dma_start(ctxT_raw, A["ctxT"][0]).then_inc(s_ctx, 16)
            t_ctx = (s_ctx, 16)
            t_kv = loaded("wkv0", small_raw, A["wkv0"])
            t_bq = loaded("bq0", bq[:, :], A["bq0"])
            t_bk = loaded("bk0", bk[:, :], A["bk0"])
            t_bv = loaded("bv0", bv[:, :], A["bv0"].broadcast_to([P, P]))
            t_bo = loaded("bo0", bo[:, :], A["bo0"].broadcast_to([P, D]))
            for b in range(HB, B):
                x_ready[b] = load(x[:, b, :], A["x"][b], s_x[b])

            t_zero = []
            for hi, lo in vp:
                for half_ in (hi, lo):
                    t_zero.append(pool.did(nc.gpsimd.memset(half_[:, :, :].bitcast(F32), 0.0)))
            dve.wait(t_const)
            t_sel = dve.did(nc.vector.tensor_copy(
                sel[:, :, :], consts[:, C_SEL:C_SEL + KT * P].rearrange("p (m c) -> p m c", m=KT)))

            banks = Ring(bank[4:8])
            s_banks = bank[0:4]
            s_free = [None] * 4

            t_w = {}
            for k in range(KT):
                t_w["q"] = split(wq[0][:, k, :], wq[1][:, k, :], w_raw[:, k, :], [t_wq])
            sp.wait(t_w["q"])
            t_wo = loaded("wo0", w_raw[:, :, :], A["wo0"])
            for n in range(2):
                t_w["kv"] = split(wkv[0][:, n], wkv[1][:, n], small_raw[:, n], [t_kv])

            qT_free = kT_free = kd_free = v_free = None
            xn_free = ctx_free = None
            pr_ring, pT_ring = Ring(pr), Ring(pT)
            vp_free = [None, None]
            aT_free = None
            for half in range(2):
                t_xn = layer_norm(range(half * HB, half * HB + HB), xnA, banks, xn_free)
                for k in range(KT):
                    t_c = split(ctxT[0][:, k, :], ctxT[1][:, k, :], ctxT_raw[:, k, :], [t_ctx], ctx_free)
                if half == 0:
                    pr_ring.release(0, t_w["kv"])
                    pr_ring.release(1, t_c)
                for b in range(half * HB, half * HB + HB):
                    pool.wait(t_xn, t_bo)
                    x_ready[b] = pool.did(nc.gpsimd.tensor_tensor(x[:, b, :], x[:, b, :], bo[:, :], ALU.add))

                j, ps, free = banks.take()
                pe.wait(free, t_c, t_w["kv"])
                t = mm_group(ps[:, :], [q for k in range(KT) for q in three(
                    (wkv[0][:, 0, k, :], wkv[1][:, 0, k, :]), (ctxT[0][:, k, :], ctxT[1][:, k, :]))])
                act.wait(t, t_bk, kT_free)
                t = act.did(nc.scalar.activation(kT[0][:, :], ps[:, :], ACT.Identity, bias=bk[:, 0:1]))
                dve.wait(t)
                t_k = dve.did(nc.vector.scalar_tensor_tensor(
                    out=kT[1][:, :], in0=ps[:, :], scalar=bk[:, 0:1], in1=kT[0][:, :].bitcast(F32),
                    op0=ALU.add, op1=ALU.subtract))
                banks.release(j, t_k)
                j, ps, free = banks.take()
                pe.wait(free)
                for b in range(HB):
                    t = mm_group(ps[:, b * P:(b + 1) * P], [q for k in range(KT) for q in three(
                        (ctxT[0][:, k, b * P:(b + 1) * P], ctxT[1][:, k, b * P:(b + 1) * P]),
                        (wkv[0][:, 1, k, :], wkv[1][:, 1, k, :]))])
                ctx_free = t
                dve.wait(t, t_bv, v_free)
                t_v = dve.did(nc.vector.tensor_tensor(
                    v[:, :, :], ps[:, :].rearrange("p (b c) -> p b c", b=HB),
                    bv[:, :].unsqueeze(1).broadcast_to([P, HB, P]), ALU.add))
                banks.release(j, t_v)
                for m in range(KT):
                    j, ps, free = banks.take()
                    pe.wait(free, t_xn, t_w["q"])
                    t = mm_group(ps[:, :], [q for k in range(KT) for q in three(
                        (wq[0][:, k, m * P:(m + 1) * P], wq[1][:, k, m * P:(m + 1) * P]),
                        (xnA[0][:, k, :], xnA[1][:, k, :]))])
                    xn_free = t
                    act.wait(t, t_bq, qT_free)
                    t = act.did(nc.scalar.activation(qT[0][:, m, :], ps[:, :], ACT.Identity, bias=bq[:, m:m + 1]))
                    dve.wait(t)
                    t_q = dve.did(nc.vector.scalar_tensor_tensor(
                        out=qT[1][:, m, :], in0=ps[:, :], scalar=bq[:, m:m + 1],
                        in1=qT[0][:, m, :].bitcast(F32), op0=ALU.add, op1=ALU.subtract))
                    banks.release(j, t_q)
                for m in range(KT):
                    j, ps, free = banks.take()
                    pe.wait(free, t_k, t_sel)
                    t = mm_group(ps[:, :], [(sel[:, m, :], kT[0][:, :]), (sel[:, m, :], kT[1][:, :])])
                    kT_free = t
                    act.wait(t, kd_free)
                    for par in range(2):
                        t_h = act.did(nc.scalar.activation(kd[0][:, m, par, :], ps[:, :], ACT.Copy,
                                                           scale=mask[:, par:par + 1]))
                    dve.wait(t_h)
                    for par in range(2):
                        t_kd = dve.did(nc.vector.scalar_tensor_tensor(
                            out=kd[1][:, m, par, :], in0=ps[:, :], scalar=mask[:, par:par + 1],
                            in1=kd[0][:, m, par, :].bitcast(F32), op0=ALU.mult, op1=ALU.subtract))
                    banks.release(j, t_kd)
                if half == 0:
                    for k in range(KT):
                        t_w["o"] = split(wo[0][:, k, :], wo[1][:, k, :], w_raw[:, k, :], [t_wo])
                    sp.wait(t_w["o"])
                    ctxT_raw = w_raw
                    nc.sync.dma_start(ctxT_raw[:, :, :], A["ctxT"][1]).then_inc(s_ctx, 16)
                    t_ctx = (s_ctx, 32)

                steps = [(b, mp) for b in range(HB) for mp in range(2)]
                state = {}

                def scores(i):
                    b, mp = steps[i]
                    tok = slice(b * P, (b + 1) * P)
                    ts = [None] * 4
                    for mi in range(2):
                        m = 2 * mp + mi
                        for n in range(3):
                            qs, ks = (0, 0, 1)[n], (0, 1, 0)[n]
                            for r in range(4):
                                rows = slice(32 * r, 32 * r + 32)
                                pe.wait(s_free[r], t_q, t_kd)
                                ins = nc.tensor.matmul(
                                    s_banks[r][:, mi * 256:(mi + 1) * 256], qT[qs][rows, m, tok],
                                    kd[ks][rows, m, :, tok], start=(n == 0), stop=(n == 2))
                                if mi == 1 and n == 2:
                                    ts[r] = pe.did(ins)
                    state[i] = {"s": ts}

                def softmax_max(i):
                    st = state[i]
                    j, _, free = pr_ring.take()
                    st["j"], st["free"] = j, free
                    for r in range(4):
                        dve.wait(st["s"][r])
                        t = dve.did(nc.vector.tensor_reduce(
                            mx[j][:, 4 * r:4 * r + 4], s_banks[r][:, :].rearrange("p (h k) -> p h k", h=4),
                            AX.X, ALU.max))
                    dve.wait(t)
                    st["nb"] = dve.did(nc.vector.tensor_scalar(nb[j][:, :], mx[j][:, :], -SCALE0, None, ALU.mult))

                def softmax_exp(i):
                    st = state[i]
                    j = st["j"]
                    act.wait(st["nb"], st["free"])
                    for r in range(4):
                        for h in range(4):
                            n = 4 * r + h
                            t = act.did(nc.scalar.activation(
                                pr[j][:, n, :], s_banks[r][:, h * P:(h + 1) * P], ACT.Exp,
                                bias=nb[j][:, n:n + 1], scale=SCALE0, accum_out=sm[j][:, n:n + 1]))
                        s_free[r] = t
                    st["e"] = t

                def softmax_norm(i):
                    st = state[i]
                    j = st["j"]
                    dve.wait(st["e"])
                    t = dve.did(nc.vector.reciprocal(ri[j][:, :], sm[j][:, :]))
                    pool.wait(t, st["e"])
                    for n in range(16):
                        t = pool.did(nc.gpsimd.tensor_scalar(pr[j][:, n, :], pr[j][:, n, :], ri[j][:, n:n + 1],
                                                             1.0, ALU.mult, ALU.mult))
                    st["p"] = t

                def values(i):
                    nonlocal aT_free
                    st = state.pop(i)
                    b, mp = steps[i]
                    j = st["j"]
                    if mp == 0:
                        w = b % 2
                        diag = [q[:, :, :].rearrange("p a c -> p (a c)") for q in vp[w]]
                        src = v[:, b, :].rearrange("p (a d) -> p a d", a=KV0)
                        dst = [bass.AP(tensor=q.tensor, offset=q.offset, ap=[list(q.ap[0]), [P + HD0, KV0], [1, HD0]])
                               for q in diag]
                        t = split(dst[0], dst[1], src, [t_v, *t_zero], vp_free[w])
                        st_v[b] = t
                        o_bank[b] = banks.take()
                    oj, ops, ofree = o_bank[b]
                    w = b % 2
                    todo = []
                    for kv in range(4):
                        tj, tps, tfree = banks.take()
                        if tj == oj:
                            tj, tps, tfree = banks.take()
                        pe.wait(tfree, st["p"], t_const)
                        for g in range(G0):
                            mi, r, par = kv // 2, 2 * (kv % 2) + g // 2, g % 2
                            ins = nc.tensor.transpose(tps[:, g * P:(g + 1) * P],
                                                      pr[j][:, 4 * r + 2 * mi + par, :], ident)
                        t = pe.did(ins)
                        if kv == 3:
                            pr_ring.release(j, t)
                        pj, pbuf, pfree = pT_ring.take()
                        t = split(pbuf[0][:, :], pbuf[1][:, :], tps[:, :], [t], pfree)
                        banks.release(tj, t)
                        todo.append((4 * mp + kv, pj, pbuf, t))
                        if kv >= 1:
                            pv(b, *todo[kv - 1])
                    pv(b, *todo[3])
                    if mp == 1:
                        t = pe.last()
                        vp_free[w] = t
                        t_a = split(aT[0][:, :], aT[1][:, :], ops[:, :], [t], aT_free)
                        banks.release(oj, t_a)
                        yj, yps, yfree = banks.take()
                        pe.wait(yfree, t_a, t_w["o"])
                        t = mm_group(yps[:, :], [q for g in range(G0) for q in three(
                            (aT[0][:, g * P:(g + 1) * P], aT[1][:, g * P:(g + 1) * P]),
                            (wo[0][:, g, :], wo[1][:, g, :]))])
                        aT_free = t
                        tile = half * HB + b
                        dve.wait(t, x_ready[tile])
                        t = dve.did(nc.vector.tensor_tensor(x[:, tile, :], yps[:, :], x[:, tile, :], ALU.add))
                        x_ready[tile] = t
                        banks.release(yj, t)

                def pv(b, kv, pj, pbuf, t):
                    w = b % 2
                    oj, ops, ofree = o_bank[b]
                    pe.wait(t, st_v[b], ofree)
                    for n, (a, c) in enumerate(three((vp[w][0][:, kv, :], vp[w][1][:, kv, :]),
                                                     (pbuf[0][:, :], pbuf[1][:, :]))):
                        ins = nc.tensor.matmul(ops[:, :], a, c, start=(kv == 0 and n == 0),
                                               stop=(kv == KV0 - 1 and n == 2))
                    pT_ring.release(pj, pe.did(ins))

                st_v, o_bank = {}, {}
                for i in range(len(steps) + 1):
                    if i < len(steps):
                        scores(i)
                        softmax_max(i)
                        softmax_exp(i)
                        softmax_norm(i)
                    if i >= 1:
                        values(i - 1)
                qT_free = kd_free = pe.last()
                v_free = dve.last()
            fence()
            scope.pop()

        with ExitStack() as phase:
            scope.append(phase)
            xnB = pair("xnB", [P, KT, HT])
            xnT = [xnA, xnB]
            CH = 512
            raw = [sb(f"wf_raw{i}", [P, 3, 2, CH]) for i in range(2)]
            wf = [pair(f"wf{i}", [P, 3, 2, CH]) for i in range(2)]
            s_act = [sb(f"silu{i}", [P, HT]) for i in range(2)]
            z = [sb(f"z{i}", [P, HT]) for i in range(2)]
            zs = [pair(f"zs{i}", [P, IT, HT]) for i in range(2)]
            gate_raw = sb("gate_raw", [P, KT, E0])
            gate = pair("gate", [P, KT, E0])
            gbias = sb("gbias", [P, E0])
            sc = sb("sc", [P, B, E0])
            mx = sb("mxf", [P, B, 8])
            mi_ = sb("mif", [P, B, 8], U32)
            mif = sb("mifl", [P, B, TOP0])
            oh = sb("ohf", [P, B, TOP0, E0])
            cw = sb("cw", [P, B, E0])
            ssum = sb("ssum", [P, B])

            land = Landing(raw, [sem(f"ld_wf{i}") for i in range(2)])
            wf_ring = Ring(wf)
            up = Ring(bank[0:4])
            down = Ring(bank[4:8])
            s_ring, z_ring, zs_ring = Ring(s_act), Ring(z), Ring(zs)

            experts = list(range(E0 + 1))
            fetched, ready, chunks = {}, {}, []

            def fetch(e):
                i, buf, free = land.take()
                sp.wait(free)
                fetched[e] = (i, buf, land.filled(i, nc.sync.dma_start(
                    buf[:, :, :, :], A["wffn"][e])))

            def queue_split(e):
                i, buf, t_in = fetched[e]
                j, dst, free = wf_ring.take()
                ready[e] = [j, dst, None]

                def piece(a, c):
                    def go():
                        t = split(dst[0][:, a, c, :], dst[1][:, a, c, :], buf[:, a, c, :], [t_in], free)
                        ready[e][2] = t
                        if (a, c) == (2, 1):
                            land.release(i, t)
                            if e + 2 <= E0:
                                fetch(e + 2)
                    return go
                chunks.extend((e, piece(a, c)) for a in range(3) for c in range(2))

            def background(n):
                for _ in range(min(n, len(chunks))):
                    chunks.pop(0)[1]()

            t_gate = loaded("gate", gate_raw[:, :, :], A["gate0"])
            t_gb = loaded("gbias", gbias[:, :], A["gbias0"].broadcast_to([P, E0]))
            fetch(0)
            fetch(1)
            queue_split(0)
            background(6)
            t_g = split(gate[0][:, :, :], gate[1][:, :, :], gate_raw[:, :, :], [t_gate])
            t_xn = [layer_norm(range(h * HB, h * HB + HB), xnT[h], down) for h in range(2)]

            def hidden(e, h):
                j, w, t_w_ = ready[e]
                zj, zbuf, zfree = zs_ring.take()
                for it in range(IT):
                    pss = []
                    for a in range(2):
                        uj, ps, free = up.take()
                        pe.wait(free, t_w_, t_xn[h])
                        def wcol(part, k):
                            return w[part][:, a, k // 2, (k % 2) * I0 + it * P:(k % 2) * I0 + (it + 1) * P]
                        t = mm_group(ps[:, :], [q for k in range(KT) for q in three(
                            (wcol(0, k), wcol(1, k)), (xnT[h][0][:, k, :], xnT[h][1][:, k, :]))])
                        pss.append((uj, ps, t))
                    (gj, gps, gt), (uj, ups, ut) = pss
                    sj, sbuf, sfree = s_ring.take()
                    act.wait(gt, sfree)
                    t_s = act.did(nc.scalar.activation(sbuf[:, :], gps[:, :], ACT.Silu))
                    up.release(gj, t_s)
                    qj, qbuf, qfree = z_ring.take()
                    dve.wait(t_s, ut, qfree)
                    t_z = dve.did(nc.vector.tensor_tensor(qbuf[:, :], ups[:, :], sbuf[:, :], ALU.mult))
                    up.release(uj, t_z)
                    s_ring.release(sj, t_z)
                    t = split(zbuf[0][:, it, :], zbuf[1][:, it, :], qbuf[:, :], [t_z], zfree)
                    z_ring.release(qj, t)
                return zj, zbuf, t

            def output(e, h, zj, zbuf, t_z):
                j, w, t_w_ = ready[e]
                for b in range(HB):
                    dj, ps, free = down.take()
                    pe.wait(free, t_z, t_w_)
                    t = mm_group(ps[:, :], [q for it in range(IT) for q in three(
                        (zbuf[0][:, it, b * P:(b + 1) * P], zbuf[1][:, it, b * P:(b + 1) * P]),
                        (w[0][:, 2, it, :], w[1][:, 2, it, :]))])
                    tile = h * HB + b
                    dve.wait(t, x_ready[tile])
                    if e == 0:
                        t = dve.did(nc.vector.tensor_tensor(x[:, tile, :], ps[:, :], x[:, tile, :], ALU.add))
                    else:
                        dve.wait(t_cw)
                        t = dve.did(nc.vector.scalar_tensor_tensor(
                            out=x[:, tile, :], in0=ps[:, :], scalar=cw[:, tile, e - 1:e],
                            in1=x[:, tile, :], op0=ALU.mult, op1=ALU.add))
                    x_ready[tile] = t
                    down.release(dj, t)
                zs_ring.release(zj, pe.last())
                if h == 1:
                    wf_ring.release(j, pe.last())

            def top(src, mx_, idx, idxf, onehot, k, n_exp, t):
                dve.wait(t)
                for b in range(B):
                    t = dve.did(nc.vector.max(mx_[:, b, :], src[:, b, :]))
                dve.wait(t)
                for b in range(B):
                    t = dve.did(nc.vector.max_index(idx[:, b, :], mx_[:, b, :], src[:, b, :]))
                dve.wait(t)
                t = dve.did(nc.vector.tensor_copy(idxf[:, :, :], idx[:, :, 0:k]))
                dve.wait(t, t_const)
                return dve.did(nc.vector.tensor_tensor(
                    onehot[:, :, :, :], idxf[:, :, :].unsqueeze(3).broadcast_to([P, B, k, n_exp]),
                    iota[:, 0:n_exp].unsqueeze(1).unsqueeze(1).broadcast_to([P, B, k, n_exp]), ALU.is_equal))

            gj, gps, free = down.take()
            pe.wait(free, t_g, t_xn[1])
            for b in range(B):
                h, cols = b // HB, slice((b % HB) * P, (b % HB + 1) * P)
                t = mm_group(gps[:, b * E0:(b + 1) * E0], [q for k in range(KT) for q in three(
                    (xnT[h][0][:, k, cols], xnT[h][1][:, k, cols]), (gate[0][:, k, :], gate[1][:, k, :]))])
            act.wait(t)
            t = act.did(nc.scalar.activation(sc[:, :, :], gps[:, 0:B * E0].rearrange("p (b e) -> p b e", b=B),
                                             ACT.Sigmoid))
            down.release(gj, t)
            dve.wait(t, t_gb)
            t = dve.did(nc.vector.tensor_tensor(
                sc[:, :, :], sc[:, :, :], gbias[:, :].unsqueeze(1).broadcast_to([P, B, E0]), ALU.add))
            t = top(sc, mx, mi_, mif, oh, TOP0, E0, t)
            dve.wait(t)
            t = dve.did(nc.vector.tensor_reduce(cw[:, :, :], oh[:, :, :, :].rearrange("p b k e -> p b e k"),
                                                AX.X, ALU.add))
            dve.wait(t)
            t = dve.did(nc.vector.tensor_tensor(cw[:, :, :], cw[:, :, :], sc[:, :, :], ALU.mult))
            t2 = dve.did(nc.vector.tensor_reduce(ssum[:, :], mx[:, :, 0:TOP0], AX.X, ALU.add))
            dve.wait(t2)
            t2 = dve.did(nc.vector.tensor_scalar(ssum[:, :], ssum[:, :], 1e-20, None, ALU.add))
            dve.wait(t2)
            t2 = dve.did(nc.vector.reciprocal(ssum[:, :], ssum[:, :]))
            dve.wait(t2)
            t_cw = dve.did(nc.vector.tensor_tensor(
                cw[:, :, :], cw[:, :, :], ssum[:, :].unsqueeze(2).broadcast_to([P, B, E0]), ALU.mult))

            before = None
            for e in experts:
                if e + 1 <= E0:
                    queue_split(e + 1)
                for h in range(2):
                    z_ = hidden(e, h)
                    if before:
                        output(*before)
                    before = (e, h, *z_)
                    if h == 0:
                        background(3)
                    else:
                        background(6)
            output(*before)
            fence()
            scope.pop()

        with ExitStack() as phase:
            scope.append(phase)
            kT = pair("k1T", [P, KV1, 2, HT])
            v = pair("v1", [P, 2, HB, D])
            head = [pair(f"w1q{i}", [P, KT, P]) for i in range(4)]
            outw = [pair(f"w1o{i}", [P, D]) for i in range(2 * UH)]
            raw = [sb(f"w1_raw{i}", [P, D]) for i in range(2)]
            qT = [pair(f"q1T{i}", [P, UH, HT]) for i in range(2)]
            pr = [sb(f"p1_{i}", [P, UH, 2 * P]) for i in range(2)]
            pT = pair("p1T", [P, 2, UH * P])
            aT = pair("a1T", [P, UH * P])
            mx = [sb(f"mx1_{i}", [P, 4 * UH]) for i in range(2)]

            land = Landing(raw, [sem(f"ld_w1{i}") for i in range(2)])
            head_ring, out_ring = Ring(head), Ring(outw)
            s_ring = Ring(bank[0:4])
            t_ring = Ring(bank[4:6])
            o_ring, y_ring = Ring(bank[6:7]), Ring(bank[7:8])
            pr_ring = Ring(pr)
            q_free = [None, None]
            pT_free = [None, None]
            aT_free = None
            xn_free = None
            kv_free = None

            def step_weights(u, b):
                n = UH * u + b + UH + 1
                w = [("wq1", n, head_ring)] if n < H1 else []
                if b >= 2 and u + 1 < UNITS:
                    w += [("wo1", UH * (u + 1) + 2 * (b - 2) + h, out_ring) for h in range(2)]
                return w

            stream = []
            for half in range(2):
                stream += [("wk1", g, head_ring) for g in range(KV1)]
                stream += [("wv1", k, out_ring) for k in range(KT)]
                stream += [("wq1", h, head_ring) for h in range(UH)]
                stream += [("wo1", h, out_ring) for h in range(UH)]
                stream += [("wq1", UH, head_ring)]
                for u in range(UNITS):
                    for b in range(HB):
                        stream += step_weights(u, b)
            loads, splits = list(stream), []
            have = {"head": [], "out": []}

            def fetch():
                if loads:
                    name, n, ring = loads.pop(0)
                    i, buf, free = land.take()
                    sp.wait(free)
                    t = land.filled(i, nc.sync.dma_start(buf[:, :], A[name][n]))
                    splits.append((ring, i, buf, t))

            def weight():
                if not splits:
                    return
                ring, i, buf, t_in = splits.pop(0)
                j, dst, free = ring.take()
                if ring is head_ring:
                    hi, lo = (q[:, :, :].rearrange("p k c -> p (k c)") for q in dst)
                else:
                    hi, lo = (q[:, :] for q in dst)
                t = split(hi, lo, buf[:, :], [t_in], free)
                land.release(i, t)
                have["head" if ring is head_ring else "out"].append((j, dst, t))
                fetch()

            for _ in raw:
                fetch()

            def project(w, t_w_, src, t_src, dst, dst_free):
                sj, ps, free = s_ring.take()
                pe.wait(free, t_w_, *t_src)
                t = mm_group(ps[:, :], [q for k in range(KT) for q in three(
                    (w[0][:, k, :], w[1][:, k, :]), (src[0][:, k, :], src[1][:, k, :]))])
                t2 = split(dst[0], dst[1], ps[:, :], [t], dst_free)
                s_ring.release(sj, t2)
                return t, t2

            s_ctx = [sem(f"ld_ctx1{i}") for i in range(2)]
            n_ctx = [0, 0]
            for half in range(2):
                ctxT = qT[1]
                for k in range(KT):
                    xj, xbuf, xfree = xn_ring.take()
                    sp.wait(xfree)
                    nc.sync.dma_start(xbuf[:, :], A["ctxT"][half][:, k, :]).then_inc(s_ctx[xj], 16)
                    n_ctx[xj] += 16
                    t_c = split(ctxT[0][:, k, :], ctxT[1][:, k, :], xbuf[:, :], [(s_ctx[xj], n_ctx[xj])], q_free[1])
                    xn_ring.release(xj, t_c)
                for _ in range(KV1):
                    weight()
                wk = have["head"]
                have["head"] = []
                for g in range(KV1):
                    _, t_kc = project(wk[g][1], wk[g][2], ctxT, [t_c],
                                      (kT[0][:, g, 0, :], kT[1][:, g, 0, :]), kv_free)
                for _ in range(KT):
                    weight()
                wv = have["out"]
                have["out"] = []

                def value_tiles(part, src, t_src):
                    for b in range(HB):
                        cols = slice(b * P, (b + 1) * P)
                        sj, ps, free = s_ring.take()
                        pe.wait(free, *t_src, *[w[2] for w in wv])
                        t = mm_group(ps[:, :], [q for k in range(KT) for q in three(
                            (src[0][:, k, cols], src[1][:, k, cols]), (wv[k][1][0][:, :], wv[k][1][1][:, :]))])
                        t2 = split(v[0][:, part, b, :], v[1][:, part, b, :], ps[:, :], [t], kv_free)
                        s_ring.release(sj, t2)
                    return t, t2

                t_cfree, _ = value_tiles(0, ctxT, [t_c])
                q_free[1] = t_cfree
                t_xn = layer_norm(range(half * HB, half * HB + HB), xnA, t_ring, xn_free)
                for g in range(KV1):
                    t, t_kx = project(wk[g][1], wk[g][2], xnA, [t_xn],
                                      (kT[0][:, g, 1, :], kT[1][:, g, 1, :]), kv_free)
                    head_ring.release(wk[g][0], t)
                t, t_kv = value_tiles(1, xnA, [t_xn])
                for k in range(KT):
                    out_ring.release(wv[k][0], t)

                steps = [(u, b) for u in range(UNITS) for b in range(HB)]
                state, t_qs = {}, {}

                def query(u, h):
                    nonlocal xn_free
                    j, w, t_w_ = have["head"].pop(0)
                    dst = qT[u % 2]
                    t, t2 = project(w, t_w_, xnA, [t_xn], (dst[0][:, h, :], dst[1][:, h, :]), q_free[u % 2])
                    head_ring.release(j, t)
                    xn_free = t
                    t_qs[u] = t2

                def scores(i):
                    u, b = steps[i]
                    g = u * UH // (H1 // KV1)
                    tok = slice(b * P, (b + 1) * P)
                    q = qT[u % 2]
                    st = state[i] = {"s": []}
                    for pr_ in range(UH // 2):
                        sj, ps, free = s_ring.take()
                        pe.wait(free, t_qs[u], t_kv)
                        for hh in range(2):
                            h = 2 * pr_ + hh
                            t = mm_group(ps[:, hh * 2 * P:(hh + 1) * 2 * P], three(
                                (q[0][:, h, tok], q[1][:, h, tok]),
                                (kT[0][:, g, :, tok], kT[1][:, g, :, tok])))
                        st["s"].append((sj, ps, t))
                    if b == HB - 1:
                        q_free[u % 2] = t

                def softmax_max(i):
                    st = state[i]
                    j, _, free = pr_ring.take()
                    st["j"], st["free"] = j, free
                    m = mx[j]
                    for n, (_, ps, t) in enumerate(st["s"]):
                        dve.wait(t)
                        t = dve.did(nc.vector.tensor_reduce(
                            m[:, 2 * n:2 * n + 2], ps[:, :].rearrange("p (h k) -> p h k", h=2), AX.X, ALU.max))
                    dve.wait(t)
                    st["nb"] = dve.did(nc.vector.tensor_scalar(m[:, UH:2 * UH], m[:, 0:UH], -SCALE1, None, ALU.mult))

                def softmax_exp(i):
                    st = state[i]
                    j = st["j"]
                    m = mx[j]
                    act.wait(st["nb"], st["free"])
                    for n, (sj, ps, _) in enumerate(st["s"]):
                        for hh in range(2):
                            h = 2 * n + hh
                            t = act.did(nc.scalar.activation(
                                pr[j][:, h, :], ps[:, hh * 2 * P:(hh + 1) * 2 * P], ACT.Exp,
                                bias=m[:, UH + h:UH + h + 1], scale=SCALE1,
                                accum_out=m[:, 2 * UH + h:2 * UH + h + 1]))
                        s_ring.release(sj, t)
                    st["e"] = t

                def softmax_norm(i):
                    st = state[i]
                    j = st["j"]
                    m = mx[j]
                    dve.wait(st["e"])
                    t = dve.did(nc.vector.reciprocal(m[:, 3 * UH:4 * UH], m[:, 2 * UH:3 * UH]))
                    pool.wait(t, st["e"])
                    for h in range(UH):
                        t = pool.did(nc.gpsimd.tensor_scalar(
                            pr[j][:, h, :], pr[j][:, h, :], m[:, 3 * UH + h:3 * UH + h + 1],
                            1.0, ALU.mult, ALU.mult))
                    st["p"] = t

                def turn(i):
                    st = state[i]
                    st["pT"] = []
                    for part in range(2):
                        tj, ps, free = t_ring.take()
                        pe.wait(free, st["p"], t_const)
                        for h in range(UH):
                            ins = nc.tensor.transpose(ps[:, h * P:(h + 1) * P],
                                                      pr[st["j"]][:, h, part * P:(part + 1) * P], ident)
                        t = pe.did(ins)
                        t2 = split(pT[0][:, part, :], pT[1][:, part, :], ps[:, :], [t], pT_free[part])
                        t_ring.release(tj, t2)
                        st["pT"].append(t2)
                    pr_ring.release(st["j"], t)

                def attend(i):
                    nonlocal aT_free
                    st = state[i]
                    u, b = steps[i]
                    g = u * UH // (H1 // KV1)
                    oj, ps, free = o_ring.take()
                    pe.wait(free)
                    prs = []
                    for part in range(2):
                        vv = tuple(q[:, part, b, g * P:(g + 1) * P] for q in v)
                        prs += three(vv, (pT[0][:, part, :], pT[1][:, part, :]))
                    for n, (a, c) in enumerate(prs):
                        pe.wait(st["pT"][n // 3])
                        ins = nc.tensor.matmul(ps[:, :], a, c, start=(n == 0), stop=(n == 5))
                        if n % 3 == 2:
                            t = pT_free[n // 3] = pe.did(ins)
                    t2 = split(aT[0][:, :], aT[1][:, :], ps[:, :], [t], aT_free)
                    o_ring.release(oj, t2)
                    st["a"] = t2

                def project_out(i):
                    nonlocal aT_free
                    st = state.pop(i)
                    u, b = steps[i]
                    if b == 0:
                        wos[u] = [have["out"].pop(0) for _ in range(UH)]
                    ws = wos[u]
                    yj, ps, free = y_ring.take()
                    pe.wait(free, st["a"], *[w[2] for w in ws])
                    t = mm_group(ps[:, :], [q for h in range(UH) for q in three(
                        (aT[0][:, h * P:(h + 1) * P], aT[1][:, h * P:(h + 1) * P]),
                        (ws[h][1][0][:, :], ws[h][1][1][:, :]))])
                    aT_free = t
                    if b == HB - 1:
                        for w in ws:
                            out_ring.release(w[0], t)
                    tile = half * HB + b
                    dve.wait(t, x_ready[tile])
                    t = dve.did(nc.vector.tensor_tensor(x[:, tile, :], ps[:, :], x[:, tile, :], ALU.add))
                    x_ready[tile] = t
                    y_ring.release(yj, t)

                wos = {}
                for h in range(2 * UH):
                    weight()
                for h in range(UH):
                    query(0, h)
                weight()
                for i in range(len(steps) + 2):
                    u, b = steps[i] if i < len(steps) else (UNITS, 0)
                    if i < len(steps):
                        scores(i)
                        softmax_max(i)
                    if 1 <= i <= len(steps):
                        turn(i - 1)
                    if i < len(steps):
                        softmax_exp(i)
                        if u + 1 < UNITS:
                            query(u + 1, b)
                    if i >= 2:
                        project_out(i - 2)
                    if i < len(steps):
                        for _ in step_weights(u, b):
                            weight()
                        softmax_norm(i)
                    if 1 <= i <= len(steps):
                        attend(i - 1)
                kv_free = pe.last()
            fence()
            scope.pop()

        with ExitStack() as phase:
            scope.append(phase)
            xnB = pair("xnB2", [P, KT, HT])
            xnT = [xnA, xnB]
            wm_raw, wm = sb("wm_raw", [P, KT, D]), pair("wm", [P, KT, D])
            ws_raw, ws = sb("ws_raw", [P, KT, SMALL]), pair("ws", [P, KT, SMALL])
            lb_raw, lb = sb("lb_raw", [P, D]), pair("lb", [P, D])
            vecs = sb("vecs", [P, 3 * G1 + E1])
            gw2 = sb("gw2", [P, E1, G1])
            h_ = sb("h_", [P, B, G1])
            hc = sb("hc", [P, B, G1])
            prod = sb("prod", [P, B, E1, G1])
            tmp = sb("tmp", [P, B, P])
            st1 = sb("st1", [P, B])
            st2 = sb("st2", [P, B])
            gates = sb("gates", [P, B, E1])
            mx = sb("mxg", [P, B, 8])
            mi_ = sb("mig", [P, B, 8], U32)
            mif = sb("migf", [P, B, TOP1])
            oh = sb("ohg", [P, B, TOP1, E1])
            gk = sb("gk", [P, B, TOP1])
            allowed = sb("allowed", [P, TOP1, E1])
            w1 = sb("w1g", [P, B, E1])
            lo_a = [pair(f"loa{i}", [P, P]) for i in range(2)]

            t_m = loaded("wm", wm_raw[:, :, :], A["wm1"])
            t_s = loaded("ws", ws_raw[:, :, :], A["ws1"])
            t_l = loaded("lb", lb_raw[:, :], A["lb1"])
            t_vec = loaded("vecs", vecs[:, :], A["vecs1"].broadcast_to([P, 3 * G1 + E1]))
            t_gw2 = loaded("gw2", gw2[:, :, :], A["gw2"].broadcast_to([P, E1, G1]))
            for k in range(KT):
                t_ws = split(ws[0][:, k, :], ws[1][:, k, :], ws_raw[:, k, :], [t_s])
            lo_ring = Ring(bank[0:2])
            t_xn = [layer_norm(range(h * HB, h * HB + HB), xnT[h], lo_ring) for h in range(2)]
            for k in range(KT):
                t_wm = split(wm[0][:, k, :], wm[1][:, k, :], wm_raw[:, k, :], [t_m])
            t_lb = split(lb[0][:, :], lb[1][:, :], lb_raw[:, :], [t_l])

            small_banks = bank[2:5]
            t_small = []
            for b in range(B):
                h, cols = b // HB, slice((b % HB) * P, (b % HB + 1) * P)
                ps = small_banks[b // 3][:, (b % 3) * SMALL:(b % 3 + 1) * SMALL]
                pe.wait(t_xn[h], t_ws)
                t_small.append(mm_group(ps, [q for k in range(KT) for q in three(
                    (xnT[h][0][:, k, cols], xnT[h][1][:, k, cols]), (ws[0][:, k, :], ws[1][:, k, :]))]))
            for n in range(3):
                tiles = list(range(3 * n, min(3 * n + 3, B)))
                k = len(tiles)
                src = small_banks[n][:, 0:k * SMALL].rearrange("p (b c) -> p b c", b=k)
                bs = slice(tiles[0], tiles[0] + k)
                dve.wait(t_small[tiles[-1]], t_vec)
                t_h = dve.did(nc.vector.tensor_tensor(
                    h_[:, bs, :], src[:, :, P:SMALL],
                    vecs[:, 0:G1].unsqueeze(1).broadcast_to([P, k, G1]), ALU.add))
                act.wait(t_h)
                t_tmp = act.did(nc.scalar.activation(tmp[:, bs, :], src[:, :, 0:P], ACT.Copy))

            main_ring = Ring(bank[5:8])

            def dense(b):
                h, cols = b // HB, slice((b % HB) * P, (b % HB + 1) * P)
                mj, ps, free = main_ring.take()
                pe.wait(free, t_wm)
                t = mm_group(ps[:, :], [q for k in range(KT) for q in three(
                    (xnT[h][0][:, k, cols], xnT[h][1][:, k, cols]), (wm[0][:, k, :], wm[1][:, k, :]))])
                dve.wait(t, x_ready[b])
                x_ready[b] = dve.did(nc.vector.tensor_tensor(x[:, b, :], ps[:, :], x[:, b, :], ALU.add))
                main_ring.release(mj, x_ready[b])

            dense_left = list(range(B))
            routed = [0]

            def bc(ap, n):
                return ap.unsqueeze(2).broadcast_to([P, B, n])

            def bv_(k0, n):
                return vecs[:, k0:k0 + n].unsqueeze(1).broadcast_to([P, B, n])

            def v_(ins):
                t = dve.did(ins)
                routed[0] += 1
                if dense_left and routed[0] % 3 == 0:
                    dense(dense_left.pop(0))
                dve.wait(t)
                return t

            TT, TS = nc.vector.tensor_tensor, nc.vector.tensor_scalar
            dve.wait(t_h)
            v_(nc.vector.tensor_reduce(st1[:, :], h_[:, :, :], AX.X, ALU.add))
            v_(TS(st1[:, :], st1[:, :], 1.0 / G1, None, ALU.mult))
            v_(TT(h_[:, :, :], h_[:, :, :], bc(st1[:, :], G1), ALU.subtract))
            v_(TT(hc[:, :, :], h_[:, :, :], h_[:, :, :], ALU.mult))
            t = v_(nc.vector.tensor_reduce(st2[:, :], hc[:, :, :], AX.X, ALU.add))
            act.wait(t)
            t = act.did(nc.scalar.activation(st2[:, :], st2[:, :], ACT.Sqrt, bias=eps, scale=1.0 / G1))
            dve.wait(t)
            v_(nc.vector.reciprocal(st2[:, :], st2[:, :]))
            v_(TT(h_[:, :, :], h_[:, :, :], bc(st2[:, :], G1), ALU.mult))
            v_(TT(h_[:, :, :], h_[:, :, :], bv_(G1, G1), ALU.mult))
            v_(TT(h_[:, :, :], h_[:, :, :], bv_(2 * G1, G1), ALU.add))
            v_(TS(h_[:, :, :], h_[:, :, :], 0.0, None, ALU.max))
            dve.wait(t_gw2)
            v_(TT(prod[:, :, :, :], h_[:, :, :].unsqueeze(2).broadcast_to([P, B, E1, G1]),
                  gw2[:, :, :].unsqueeze(1).broadcast_to([P, B, E1, G1]), ALU.mult))
            v_(nc.vector.tensor_reduce(gates[:, :, :], prod[:, :, :, :], AX.X, ALU.add))
            t = v_(TT(gates[:, :, :], gates[:, :, :], bv_(3 * G1, E1), ALU.add))
            t_oh = top(gates, mx, mi_, mif, oh, TOP1, E1, t)
            v_(TT(gk[:, :, :], mx[:, :, 0:TOP1], mx[:, :, 0:1].broadcast_to([P, B, TOP1]), ALU.subtract))
            act.wait(dve.last())
            t = act.did(nc.scalar.activation(gk[:, :, :], gk[:, :, :], ACT.Exp))
            cps = bank[0]
            pe.wait(t_oh, lo_ring.reader[0], t_const)
            t_cnt = mm_group(cps[:, 0:TOP1 * E1], [(ones, oh[:, b, :, :].rearrange("p k e -> p (k e)"))
                                                   for b in range(B)])
            dve.wait(t_cnt)
            v_(TS(allowed[:, :, :], cps[:, 0:TOP1 * E1].rearrange("p (k e) -> p k e", k=TOP1),
                  float(CAPACITY), 1.0 / R1, ALU.is_le, ALU.mult))
            dve.wait(t)
            v_(nc.vector.tensor_reduce(st1[:, :], gk[:, :, :], AX.X, ALU.add))
            v_(nc.vector.reciprocal(st1[:, :], st1[:, :]))
            v_(TT(gk[:, :, :], gk[:, :, :], bc(st1[:, :], TOP1), ALU.mult))
            for k in range(TOP1):
                v_(TT(oh[:, :, k, :], oh[:, :, k, :], bc(gk[:, :, k], E1), ALU.mult))
                v_(TT(oh[:, :, k, :], oh[:, :, k, :],
                      allowed[:, k, :].unsqueeze(1).broadcast_to([P, B, E1]), ALU.mult))
            v_(TT(w1[:, :, :], oh[:, :, 0, :], oh[:, :, 1, :], ALU.add))
            dve.wait(t_tmp)
            t4 = tmp[:, :, :].rearrange("p b (e r) -> p b e r", e=E1)
            t_w1 = v_(TT(t4, t4, w1[:, :, :].unsqueeze(3).broadcast_to([P, B, E1, R1]), ALU.mult))
            while dense_left:
                dense(dense_left.pop(0))
            turn_ring, lora_ring, la_ring = Ring(bank[0:2]), Ring(bank[2:5]), Ring(lo_a)
            turn_ring.release(0, t_w1)
            s_out = sem("stored")
            for b in range(B):
                tj, ps, free = turn_ring.take()
                pe.wait(free, t_w1)
                t = pe.did(nc.tensor.transpose(ps[:, 0:P], tmp[:, b, :], ident))
                aj, abuf, afree = la_ring.take()
                t = split(abuf[0][:, :], abuf[1][:, :], ps[:, 0:P], [t], afree)
                turn_ring.release(tj, t)
                rj, ps, free = lora_ring.take()
                pe.wait(free, t, t_lb)
                t = mm_group(ps[:, :], three((abuf[0][:, :], abuf[1][:, :]), (lb[0][:, :], lb[1][:, :])))
                la_ring.release(aj, t)
                dve.wait(t, x_ready[b])
                t = dve.did(nc.vector.tensor_tensor(x[:, b, :], ps[:, :], x[:, b, :], ALU.add))
                lora_ring.release(rj, t)
                sp.wait(t)
                nc.sync.dma_start(out[b], x[:, b, :]).then_inc(s_out, 16)
            nc.sync.wait_ge(s_out, 16 * B)
            scope.pop()


def constants():
    import numpy as np

    c = np.zeros((P, CONST), np.float32)
    c[:, C_ID:C_ID + P] = np.eye(P)
    for m in range(KT):
        for col in range(P):
            j, d = col // (G0 * HD0), col % HD0
            c[(2 * m + j) * HD0 + d, C_SEL + m * P + col] = 1.0
    c[:, C_ONES:C_ONES + P] = 1.0
    for p in range(P):
        c[p, C_MASK + (p // HD0) % 2] = 1.0
    c[:, C_IOTA:C_IOTA + 16] = np.arange(16)
    c[:, C_EPS] = LN_EPS
    return c


def layout(i):
    import numpy as np

    def rows(w):
        return w.reshape(w.shape[0] // P, P, w.shape[1]).transpose(1, 0, 2)

    def row(v):
        return v.reshape(1, -1)

    a = {k: np.asarray(v) for k, v in i.items()}
    wffn = np.stack([
        np.stack([rows(w.T).reshape(P, 2, 512) for w in (g, u, d)], axis=1)
        for g, u, d in [(a["L0_ffn_Sg"], a["L0_ffn_Su"], a["L0_ffn_Sd"]),
                        *zip(a["L0_ffn_Wg"], a["L0_ffn_Wu"], a["L0_ffn_Wd"])]])
    by_head = lambda w: rows(w).reshape(P, KT, w.shape[1] // P, P).transpose(2, 0, 1, 3).reshape(-1, P, D)
    lora_a = a["L1_ffn_lora_A"].transpose(1, 0, 2).reshape(D, E1 * R1)
    laid = {
        "consts": constants(),
        "x": a["x"],
        "ctxT": rows(a["ctx_4096"].reshape(B * P, D).T).reshape(P, KT, 2, HT).transpose(2, 0, 1, 3),
        "wq0": rows(a["L0_xattn_Wq"]),
        "wkv0": np.stack([rows(a["L0_xattn_Wk"]), rows(a["L0_xattn_Wv"])], axis=1),
        "wo0": a["L0_xattn_Wo"].reshape(KV0, G0, HD0, D).transpose(0, 2, 1, 3).reshape(P, G0, D),
        "bq0": a["L0_xattn_bq"].reshape(KT, P).T,
        "bk0": a["L0_xattn_bk"].reshape(P, 1),
        "bv0": row(a["L0_xattn_bv"]),
        "bo0": row(a["L0_xattn_bo"]),
        "gate0": rows(a["L0_ffn_gate_w"].T),
        "gbias0": row(a["L0_ffn_bias"]),
        "wffn": wffn,
        "wk1": by_head(a["L1_xattn_Wk"]),
        "wv1": a["L1_xattn_Wv"].reshape(KT, P, D),
        "wq1": by_head(a["L1_xattn_Wq"]),
        "wo1": a["L1_xattn_Wo"].reshape(H1, P, D),
        "wm1": rows(a["L1_ffn_weight"].T),
        "ws1": rows(np.concatenate([lora_a, a["L1_ffn_gw1"].T], axis=1)),
        "lb1": a["L1_ffn_lora_B"].reshape(E1 * R1, D),
        "vecs1": row(np.concatenate([a["L1_ffn_gb1"], a["L1_ffn_ln_gamma"], a["L1_ffn_ln_beta"], a["L1_ffn_gb2"]])),
        "gw2": a["L1_ffn_gw2"].reshape(1, E1, G1),
    }
    return {k: np.ascontiguousarray(v) for k, v in laid.items()}


def kernel(**inputs):
    import concourse.bacc as bacc
    from concourse.bass_utils import run_bass_kernel_spmd

    laid = layout(inputs)
    nc = bacc.Bacc("TRN2", target_bir_lowering=False, num_devices=1)
    A = {name: nc.dram_tensor("in_" + name, a.shape, mybir.dt.from_np(a.dtype), kind="ExternalInput").ap()
         for name, a in laid.items()}
    out = nc.dram_tensor("out", (B, P, D), F32, kind="ExternalOutput").ap()
    layers_kernel(nc, A, out)
    r = run_bass_kernel_spmd(nc, [{"in_" + name: a for name, a in laid.items()}], core_ids=[0])
    return r.results[0]["out"]
```

```python
from contextlib import ExitStack

import concourse.bass as bass
from concourse import mybir

F32 = mybir.dt.float32
F32R = mybir.dt.float32r
U32 = mybir.dt.uint32
ALU = mybir.AluOpType
ACT = mybir.ActivationFunctionType
AX = mybir.AxisListType

P = 128
B = 8
D = 512
KT = D // P
HB = B // 2
HT = HB * P
LN_EPS = 1e-5

H0, KV0, HD0 = 32, 8, 16
G0 = H0 // KV0
E0, TOP0, I0 = 16, 4, 256
IT = I0 // P
H1, KV1 = 32, 4
UH = 4
UNITS = H1 // UH
SCALE0 = 0.25
SCALE1 = float(P) ** -0.5
E1, TOP1, R1 = 8, 2, 16
G1 = 4 * E1
SMALL = P + G1
CAPACITY = int(3.0 * B * P / E1)

C_ID, C_MASK, C_IOTA, C_EPS = 0, 128, 132, 148
CONST = 149


class Queue:

    def __init__(self, eng, sem):
        self.eng, self.sem, self.count, self.seen = eng, sem, 0, {}

    def wait(self, *tokens):
        for t in tokens:
            if t is None:
                continue
            sem, value = t
            if self.seen.get(sem.name, 0) < value:
                self.eng.wait_ge(sem, value)
                self.seen[sem.name] = value

    def did(self, ins):
        self.count += 1
        ins.then_inc(self.sem, 1)
        return (self.sem, self.count)

    def last(self):
        return (self.sem, self.count)


class Ring:

    def __init__(self, bufs):
        self.bufs, self.reader, self.at = bufs, [None] * len(bufs), 0
        self.taken = [False] * len(bufs)

    def take(self):
        i = self.at % len(self.bufs)
        self.at += 1
        assert not self.taken[i], "taken before its last reader is known"
        self.taken[i] = True
        return i, self.bufs[i], self.reader[i]

    def release(self, i, token):
        self.reader[i], self.taken[i] = token, False


class Landing(Ring):

    def __init__(self, bufs, sems):
        super().__init__(bufs)
        self.sems, self.fills = sems, [0] * len(bufs)

    def filled(self, i, ins):
        self.fills[i] += 1
        ins.then_inc(self.sems[i], 16)
        return (self.sems[i], 16 * self.fills[i])


def three(hi_lo_a, hi_lo_b):
    (ah, al), (bh, bl) = hi_lo_a, hi_lo_b
    return (ah, bh), (ah, bl), (al, bh)


def layers_kernel(nc, A, out):
    with ExitStack() as whole:
        scope = [whole]

        def sb(name, shape, dt=F32):
            return scope[-1].enter_context(nc.sbuf_tensor(name, shape, dt))

        def pair(name, shape):
            return sb(name + "_hi", shape, F32R), sb(name + "_lo", shape, F32R)

        def sem(name):
            return whole.enter_context(nc.semaphore(name))

        pe = Queue(nc.tensor, sem("pe_done"))
        act = Queue(nc.scalar, sem("act_done"))
        dve = Queue(nc.vector, sem("dve_done"))
        pool = Queue(nc.gpsimd, sem("pool_done"))
        sp = Queue(nc.sync, sem("sp_unused"))

        def load(dst, src, sem_):
            nc.sync.dma_start(dst, src).then_inc(sem_, 16)
            return (sem_, 16)

        def loaded(name, dst, src):
            return load(dst, src, sem("ld_" + name))

        def split(hi, lo, src, ready, free=None, hi_on=None):
            if hi_on is pool:
                pool.wait(*ready, free)
                t = pool.did(nc.gpsimd.tensor_copy(hi, src))
            else:
                act.wait(*ready, free)
                t = act.did(nc.scalar.activation(hi, src, ACT.Copy))
            dve.wait(t, *ready, free)
            return dve.did(nc.vector.tensor_tensor(lo, src, hi.bitcast(F32), ALU.subtract))

        def mm_group(dst, pairs, mark=True):
            pairs = list(pairs)
            for n, (a, b) in enumerate(pairs):
                ins = nc.tensor.matmul(dst, a, b, start=(n == 0), stop=(n == len(pairs) - 1))
            return pe.did(ins) if mark else None

        def fence():
            tokens = [q.last() for q in (pe, act, dve, pool) if q.count]
            for q in (pe, act, dve, pool, sp):
                q.wait(*tokens)

        bank = [whole.enter_context(nc.psum_tensor(f"bank{i}", [P, 512], F32)) for i in range(8)]

        x = sb("x", [P, B, D])
        x_ready = [None] * B
        xnA = pair("xnA", [P, KT, HT])
        consts = sb("consts", [P, CONST])
        ident = consts[:, C_ID:C_ID + P]
        eps = consts[:, C_EPS:C_EPS + 1]
        iota = consts[:, C_IOTA:C_IOTA + 16]
        stats = sb("stats", [P, B, 6])
        moments = sb("moments", [P, B, 2])
        rstd = sb("rstd", [P, B])
        xn = [sb(f"xn{i}", [P, D]) for i in range(2)]
        xn_ring = Ring(xn)

        t_const = loaded("consts", consts[:, :], A["consts"])
        s_x = [sem(f"ld_x{b}") for b in range(B)]

        def layer_norm(tiles, dest, banks, dest_free=None):
            b0 = tiles[0]
            for b in tiles:
                dve.wait(x_ready[b])
                t = dve.did(nc.vector.bn_stats(stats[:, b, :], x[:, b, :]))
                dve.wait(t)
                t = dve.did(nc.vector.bn_aggr(moments[:, b, :], stats[:, b, :]))
            act.wait(t, t_const)
            r = rstd[:, b0:b0 + len(tiles)]
            t = act.did(nc.scalar.activation(r, moments[:, b0:b0 + len(tiles), 1], ACT.Sqrt, bias=eps))
            dve.wait(t)
            t_r = dve.did(nc.vector.reciprocal(r, r))
            for n, b in enumerate(tiles):
                i, buf, free = xn_ring.take()
                dve.wait(t_r, free)
                t = dve.did(nc.vector.tensor_scalar(buf[:, :], x[:, b, :], moments[:, b, 0:1],
                                                    rstd[:, b:b + 1], ALU.subtract, ALU.mult))
                j, ps, ps_free = banks.take()
                pe.wait(t, t_const, ps_free)
                for k in range(KT):
                    ins = nc.tensor.transpose(ps[:, k * P:(k + 1) * P], buf[:, k * P:(k + 1) * P], ident)
                t = pe.did(ins)
                xn_ring.release(i, t)
                cols = slice((b % HB) * P, (b % HB + 1) * P)
                ps3 = ps[:, :].rearrange("p (k t) -> p k t", k=KT)
                t = split(dest[0][:, :, cols], dest[1][:, :, cols], ps3, [t], dest_free)
                banks.release(j, t)
            return t

        with ExitStack() as phase:
            scope.append(phase)
            ctxT = pair("ctx0", [P, KT, HT])
            w_raw = sb("w0_raw", [P, KT, D])
            wq = pair("wq0", [P, KT, D])
            wkv = pair("wkv0", [P, 2, KT, P])
            wo = pair("wo0", [P, KT, D])
            sel = sb("sel", [P, KT, P], F32R)
            qT = pair("q0T", [P, KT, HT])
            kT = pair("k0T", [P, HT])
            kd = [pair(f"k0d{i}", [P, KT, G0, P]) for i in range(2)]
            v = sb("v0", [P, HB, P])
            vp = [pair(f"v0p{i}", [P, KV0, P]) for i in range(2)]
            bq = sb("bq0", [P, KT])
            bk = sb("bk0", [P, 1])
            bv = sb("bv0", [P, P])
            bo = sb("bo0", [P, D])
            ctxT_raw = sb("ctx0_raw", [P, KT, HT])
            PR = 4
            pr = sb("p0", [P, PR, G0, P])
            sx = sb("sx0", [P, PR, 4, G0])
            pT = [pair(f"p0T{i}", [P, HT]) for i in range(2)]
            aT = pair("a0T", [P, G0 * P])

            small_raw = pr[:, 0:2, :, :]
            sel_raw = pr[:, 2, :, :]
            mask = consts[:, C_MASK:C_MASK + G0]
            s_ctx = sem("ld_ctx0")

            for b in range(HB):
                x_ready[b] = load(x[:, b, :], A["x"][b], s_x[b])
            t_wq = loaded("wq0", w_raw[:, :, :], A["wq0"])
            nc.sync.dma_start(ctxT_raw[:, :, :], A["ctxT"][0]).then_inc(s_ctx, 16)
            t_ctx = (s_ctx, 16)
            t_kv = loaded("wkv0", small_raw, A["wkv0"])
            t_bq = loaded("bq0", bq[:, :], A["bq0"])
            t_bk = loaded("bk0", bk[:, :], A["bk0"])
            t_bv = loaded("bv0", bv[:, :], A["bv0"].broadcast_to([P, P]))
            t_bo = loaded("bo0", bo[:, :], A["bo0"].broadcast_to([P, D]))
            for b in range(HB, B):
                x_ready[b] = load(x[:, b, :], A["x"][b], s_x[b])

            t_zero = []
            for hi, lo in vp:
                for half_ in (hi, lo):
                    t_zero.append(pool.did(nc.gpsimd.memset(half_[:, :, :].bitcast(F32), 0.0)))
            t_sel_raw = loaded("sel", sel_raw, A["sel"])
            dve.wait(t_sel_raw)
            t_sel = dve.did(nc.vector.tensor_copy(sel[:, :, :], sel_raw))

            banks = Ring(bank[0:4])
            s_ring, t_ring = Ring(bank[0:3]), Ring(bank[3:5])
            o_ring, y_ring = Ring(bank[5:6]), Ring(bank[6:8])

            t_w = {}
            for k in range(KT):
                t_w["q"] = split(wq[0][:, k, :], wq[1][:, k, :], w_raw[:, k, :], [t_wq])
            sp.wait(t_w["q"])
            t_wo = loaded("wo0", w_raw[:, :, :], A["wo0"])
            for n in range(2):
                t_w["kv"] = split(wkv[0][:, n], wkv[1][:, n], small_raw[:, n], [t_kv])

            qT_free = kT_free = v_free = xn_free = ctx_free = aT_free = None
            pr_ring, pT_ring, kd_ring, vp_ring = Ring(range(PR)), Ring(pT), Ring(kd), Ring(vp)
            for half in range(2):
                t_xn = layer_norm(range(half * HB, half * HB + HB), xnA, banks, xn_free)
                for k in range(KT):
                    t_c = split(ctxT[0][:, k, :], ctxT[1][:, k, :], ctxT_raw[:, k, :], [t_ctx], ctx_free)
                if half == 0:
                    pr_ring.release(0, t_w["kv"])
                    pr_ring.release(1, t_w["kv"])
                    pr_ring.release(2, t_sel)
                    sp.wait(t_c)
                    nc.sync.dma_start(ctxT_raw[:, :, :], A["ctxT"][1]).then_inc(s_ctx, 16)
                    t_ctx = (s_ctx, 32)
                for b in range(half * HB, half * HB + HB):
                    pool.wait(t_xn, t_bo)
                    x_ready[b] = pool.did(nc.gpsimd.tensor_tensor(x[:, b, :], x[:, b, :], bo[:, :], ALU.add))

                j, ps, free = banks.take()
                pe.wait(free, t_c, t_w["kv"])
                t = mm_group(ps[:, :], [q for k in range(KT) for q in three(
                    (wkv[0][:, 0, k, :], wkv[1][:, 0, k, :]), (ctxT[0][:, k, :], ctxT[1][:, k, :]))])
                act.wait(t, t_bk, kT_free)
                t = act.did(nc.scalar.activation(kT[0][:, :], ps[:, :], ACT.Identity, bias=bk[:, 0:1]))
                dve.wait(t)
                t_k = dve.did(nc.vector.scalar_tensor_tensor(
                    out=kT[1][:, :], in0=ps[:, :], scalar=bk[:, 0:1], in1=kT[0][:, :].bitcast(F32),
                    op0=ALU.add, op1=ALU.subtract))
                banks.release(j, t_k)
                j, ps, free = banks.take()
                pe.wait(free)
                for b in range(HB):
                    t = mm_group(ps[:, b * P:(b + 1) * P], [q for k in range(KT) for q in three(
                        (ctxT[0][:, k, b * P:(b + 1) * P], ctxT[1][:, k, b * P:(b + 1) * P]),
                        (wkv[0][:, 1, k, :], wkv[1][:, 1, k, :]))])
                ctx_free = t
                dve.wait(t, t_bv, v_free)
                t_v = dve.did(nc.vector.tensor_tensor(
                    v[:, :, :], ps[:, :].rearrange("p (b c) -> p b c", b=HB),
                    bv[:, :].unsqueeze(1).broadcast_to([P, HB, P]), ALU.add))
                banks.release(j, t_v)
                for m in range(KT):
                    j, ps, free = banks.take()
                    pe.wait(free, t_xn, t_w["q"])
                    t = mm_group(ps[:, :], [q for k in range(KT) for q in three(
                        (wq[0][:, k, m * P:(m + 1) * P], wq[1][:, k, m * P:(m + 1) * P]),
                        (xnA[0][:, k, :], xnA[1][:, k, :]))])
                    xn_free = t
                    act.wait(t, t_bq, qT_free)
                    t = act.did(nc.scalar.activation(qT[0][:, m, :], ps[:, :], ACT.Identity, bias=bq[:, m:m + 1]))
                    dve.wait(t)
                    t_q = dve.did(nc.vector.scalar_tensor_tensor(
                        out=qT[1][:, m, :], in0=ps[:, :], scalar=bq[:, m:m + 1],
                        in1=qT[0][:, m, :].bitcast(F32), op0=ALU.add, op1=ALU.subtract))
                    banks.release(j, t_q)
                if half == 0:
                    for k in range(KT):
                        t_w["o"] = split(wo[0][:, k, :], wo[1][:, k, :], w_raw[:, k, :], [t_wo])
                for ring, first in ((s_ring, 0), (t_ring, 3)):
                    for n in range(len(ring.bufs)):
                        if first + n < 4:
                            ring.release(n, banks.reader[first + n])

                units = [(b, kv) for b in range(HB) for kv in range(KV0)]
                row, state = {}, {}

                def keys_repeat(b):
                    st = row.setdefault(b, {})
                    j, ps, free = y_ring.take()
                    pe.wait(free, t_k, t_sel)
                    cols = slice(b * P, (b + 1) * P)
                    for m in range(KT):
                        t = mm_group(ps[:, m * P:(m + 1) * P], [(sel[:, m, :], kT[0][:, cols]),
                                                                (sel[:, m, :], kT[1][:, cols])])
                    st["rep"] = (j, ps, t)
                    st["kd"] = kd_ring.take()

                def keys_mask(b, g):
                    st = row[b]
                    j, ps, t = st["rep"]
                    kj, buf, free = st["kd"]
                    src = ps[:, :].rearrange("p (m c) -> p m c", m=KT)
                    dve.wait(t, free)
                    t = dve.did(nc.vector.tensor_scalar(buf[0][:, :, g, :], src, mask[:, g:g + 1], None, ALU.mult))
                    dve.wait(t)
                    st["t_kd"] = dve.did(nc.vector.scalar_tensor_tensor(
                        out=buf[1][:, :, g, :], in0=src, scalar=mask[:, g:g + 1],
                        in1=buf[0][:, :, g, :].bitcast(F32), op0=ALU.mult, op1=ALU.subtract))
                    if g == G0 - 1:
                        y_ring.release(j, st["t_kd"])

                def values_spread(b):
                    st = row[b]
                    w, buf, free = st["vp"] = vp_ring.take()
                    dst = [bass.AP(tensor=q.tensor, offset=q.offset, ap=[list(q.ap[0]), [P + HD0, KV0], [1, HD0]])
                           for q in (h[:, :, :].rearrange("p a c -> p (a c)") for h in buf)]
                    act.wait(*t_zero)
                    st["t_v"] = split(dst[0], dst[1], v[:, b, :].rearrange("p (a d) -> p a d", a=KV0), [t_v], free)

                def scores(i):
                    b, kv = units[i]
                    rows, m = slice(64 * (kv % 2), 64 * (kv % 2) + 64), kv // 2
                    kb = row[b]["kd"][1]
                    sj, ps, free = s_ring.take()
                    pe.wait(free, t_q, row[b]["t_kd"])
                    t = mm_group(ps[:, :], three(
                        tuple(q[rows, m, b * P:(b + 1) * P] for q in qT),
                        tuple(k[rows, m, :, :] for k in kb)))
                    if kv == KV0 - 1:
                        kd_ring.release(row[b]["kd"][0], t)
                    state[i] = {"s": (sj, ps, t)}

                def softmax_max(i):
                    st = state[i]
                    sj, ps, t = st["s"]
                    j, _, free = st["pr"] = pr_ring.take()
                    dve.wait(t)
                    t = dve.did(nc.vector.tensor_reduce(sx[:, j, 0, :], ps[:, :].rearrange("p (h k) -> p h k", h=G0),
                                                        AX.X, ALU.max))
                    dve.wait(t)
                    st["nb"] = dve.did(nc.vector.tensor_scalar(sx[:, j, 1, :], sx[:, j, 0, :], -SCALE0, None, ALU.mult))

                def softmax_exp(i):
                    st = state[i]
                    sj, ps, _ = st["s"]
                    j, _, free = st["pr"]
                    act.wait(st["nb"], free)
                    for g in range(G0):
                        t = act.did(nc.scalar.activation(
                            pr[:, j, g, :], ps[:, g * P:(g + 1) * P], ACT.Exp,
                            bias=sx[:, j, 1, g:g + 1], scale=SCALE0, accum_out=sx[:, j, 2, g:g + 1]))
                    s_ring.release(sj, t)
                    st["e"] = t

                def softmax_norm(i):
                    st = state[i]
                    j = st["pr"][0]
                    dve.wait(st["e"])
                    t = dve.did(nc.vector.reciprocal(sx[:, j, 3, :], sx[:, j, 2, :]))
                    pool.wait(t, st["e"])
                    for g in range(G0):
                        t = pool.did(nc.gpsimd.tensor_scalar(pr[:, j, g, :], pr[:, j, g, :], sx[:, j, 3, g:g + 1],
                                                             1.0, ALU.mult, ALU.mult))
                    st["p"] = t

                def turn(i):
                    st = state[i]
                    j = st["pr"][0]
                    tj, ps, free = t_ring.take()
                    pe.wait(free, st["p"], t_const)
                    for g in range(G0):
                        ins = nc.tensor.transpose(ps[:, g * P:(g + 1) * P], pr[:, j, g, :], ident)
                    t = pe.did(ins)
                    pr_ring.release(j, t)
                    pj, buf, free = pT_ring.take()
                    t = split(buf[0][:, :], buf[1][:, :], ps[:, :], [t], free)
                    t_ring.release(tj, t)
                    st["pT"] = (pj, buf, t)

                def attend(i):
                    b, kv = units[i]
                    st = state.pop(i)
                    pj, buf, t = st["pT"]
                    if kv == 0:
                        row[b]["o"] = o_ring.take()
                    oj, ops, free = row[b]["o"]
                    w, vbuf, _ = row[b]["vp"]
                    pe.wait(t, row[b]["t_v"], free)
                    for n, (a_, c_) in enumerate(three((vbuf[0][:, kv, :], vbuf[1][:, kv, :]),
                                                       (buf[0][:, :], buf[1][:, :]))):
                        ins = nc.tensor.matmul(ops[:, :], a_, c_, start=(kv == 0 and n == 0),
                                               stop=(kv == KV0 - 1 and n == 2))
                    t = pe.did(ins)
                    pT_ring.release(pj, t)
                    if kv == KV0 - 1:
                        vp_ring.release(w, t)
                        row[b]["a"] = split(aT[0][:, :], aT[1][:, :], ops[:, :], [t], aT_free)
                        o_ring.release(oj, row[b]["a"])

                def project_out(b):
                    nonlocal aT_free
                    yj, yps, yfree = y_ring.take()
                    pe.wait(yfree, row[b]["a"], t_w["o"])
                    t = mm_group(yps[:, :], [q for g in range(G0) for q in three(
                        (aT[0][:, g * P:(g + 1) * P], aT[1][:, g * P:(g + 1) * P]),
                        (wo[0][:, g, :], wo[1][:, g, :]))])
                    aT_free = t
                    tile = half * HB + b
                    dve.wait(t, x_ready[tile])
                    t = dve.did(nc.vector.tensor_tensor(x[:, tile, :], yps[:, :], x[:, tile, :], ALU.add))
                    x_ready[tile] = t
                    y_ring.release(yj, t)

                keys_repeat(0)
                for g in range(G0):
                    keys_mask(0, g)
                values_spread(0)
                LAG_T, LAG_A = 2, 3
                n_units = len(units)
                for i in range(-1, n_units + LAG_A + 1):
                    b, kv = divmod(i, KV0)
                    if i + 1 < n_units:
                        scores(i + 1)
                    if 1 <= i <= n_units:
                        softmax_norm(i - 1)
                    if i + 1 < n_units:
                        softmax_max(i + 1)
                    if 0 <= i < n_units:
                        softmax_exp(i)
                    if LAG_T <= i < n_units + LAG_T:
                        turn(i - LAG_T)
                    if LAG_A <= i < n_units + LAG_A:
                        attend(i - LAG_A)
                    if 0 <= b < HB - 1:
                        if kv == 1:
                            keys_repeat(b + 1)
                        if kv == LAG_A:
                            values_spread(b + 1)
                        if 2 <= kv < 2 + G0:
                            keys_mask(b + 1, kv - 2)
                    if i > LAG_A and (i - LAG_A) % KV0 == 0:
                        project_out((i - LAG_A) // KV0 - 1)
                qT_free = kT_free = pe.last()
                v_free = dve.last()
                for n, ring in ((0, s_ring), (1, s_ring), (2, s_ring), (3, t_ring)):
                    banks.release(n, ring.reader[n % 3])
            fence()
            scope.pop()

        with ExitStack() as phase:
            scope.append(phase)
            xnB = pair("xnB", [P, KT, HT])
            xnT = [xnA, xnB]
            CH = 512
            raw = [sb(f"wf_raw{i}", [P, 3, 2, CH]) for i in range(2)]
            wf = [pair(f"wf{i}", [P, 3, 2, CH]) for i in range(2)]
            s_act = [sb(f"silu{i}", [P, HT]) for i in range(2)]
            z = [sb(f"z{i}", [P, HT]) for i in range(2)]
            zs = [pair(f"zs{i}", [P, IT, HT]) for i in range(2)]
            gate_raw = sb("gate_raw", [P, KT, E0])
            gate = pair("gate", [P, KT, E0])
            gbias = sb("gbias", [P, E0])
            sc = sb("sc", [P, B, E0])
            mx = sb("mxf", [P, B, 8])
            mi_ = sb("mif", [P, B, 8], U32)
            mif = sb("mifl", [P, B, TOP0])
            oh = sb("ohf", [P, B, TOP0, E0])
            cw = sb("cw", [P, B, E0])
            ssum = sb("ssum", [P, B])

            land = Landing(raw, [sem(f"ld_wf{i}") for i in range(2)])
            wf_ring = Ring(wf)
            up = Ring(bank[0:4])
            down = Ring(bank[4:8])
            s_ring, z_ring, zs_ring = Ring(s_act), Ring(z), Ring(zs)

            experts = list(range(E0 + 1))
            fetched, ready, chunks = {}, {}, []

            def fetch(e):
                i, buf, free = land.take()
                sp.wait(free)
                fetched[e] = (i, buf, land.filled(i, nc.sync.dma_start(
                    buf[:, :, :, :], A["wffn"][e])))

            def queue_split(e):
                i, buf, t_in = fetched[e]
                j, dst, free = wf_ring.take()
                ready[e] = [j, dst, None]

                def piece(a, c):
                    def go():
                        t = split(dst[0][:, a, c, :], dst[1][:, a, c, :], buf[:, a, c, :], [t_in], free)
                        ready[e][2] = t
                        if (a, c) == (2, 1):
                            land.release(i, t)
                            if e + 2 <= E0:
                                fetch(e + 2)
                    return go
                chunks.extend((e, piece(a, c)) for a in range(3) for c in range(2))

            def background(n):
                for _ in range(min(n, len(chunks))):
                    chunks.pop(0)[1]()

            t_gate = loaded("gate", gate_raw[:, :, :], A["gate0"])
            t_gb = loaded("gbias", gbias[:, :], A["gbias0"].broadcast_to([P, E0]))
            fetch(0)
            fetch(1)
            queue_split(0)
            background(6)
            t_g = split(gate[0][:, :, :], gate[1][:, :, :], gate_raw[:, :, :], [t_gate])
            t_xn = [layer_norm(range(h * HB, h * HB + HB), xnT[h], down) for h in range(2)]

            def hidden(e, h):
                j, w, t_w_ = ready[e]
                zj, zbuf, zfree = zs_ring.take()
                for it in range(IT):
                    pss = []
                    for a in range(2):
                        uj, ps, free = up.take()
                        pe.wait(free, t_w_, t_xn[h])
                        def wcol(part, k):
                            return w[part][:, a, k // 2, (k % 2) * I0 + it * P:(k % 2) * I0 + (it + 1) * P]
                        t = mm_group(ps[:, :], [q for k in range(KT) for q in three(
                            (wcol(0, k), wcol(1, k)), (xnT[h][0][:, k, :], xnT[h][1][:, k, :]))])
                        pss.append((uj, ps, t))
                    (gj, gps, gt), (uj, ups, ut) = pss
                    sj, sbuf, sfree = s_ring.take()
                    act.wait(gt, sfree)
                    t_s = act.did(nc.scalar.activation(sbuf[:, :], gps[:, :], ACT.Silu))
                    up.release(gj, t_s)
                    qj, qbuf, qfree = z_ring.take()
                    dve.wait(t_s, ut, qfree)
                    t_z = dve.did(nc.vector.tensor_tensor(qbuf[:, :], ups[:, :], sbuf[:, :], ALU.mult))
                    up.release(uj, t_z)
                    s_ring.release(sj, t_z)
                    t = split(zbuf[0][:, it, :], zbuf[1][:, it, :], qbuf[:, :], [t_z], zfree)
                    z_ring.release(qj, t)
                return zj, zbuf, t

            def output(e, h, zj, zbuf, t_z):
                j, w, t_w_ = ready[e]
                for b in range(HB):
                    dj, ps, free = down.take()
                    pe.wait(free, t_z, t_w_)
                    t = mm_group(ps[:, :], [q for it in range(IT) for q in three(
                        (zbuf[0][:, it, b * P:(b + 1) * P], zbuf[1][:, it, b * P:(b + 1) * P]),
                        (w[0][:, 2, it, :], w[1][:, 2, it, :]))])
                    tile = h * HB + b
                    dve.wait(t, x_ready[tile])
                    if e == 0:
                        t = dve.did(nc.vector.tensor_tensor(x[:, tile, :], ps[:, :], x[:, tile, :], ALU.add))
                    else:
                        dve.wait(t_cw)
                        t = dve.did(nc.vector.scalar_tensor_tensor(
                            out=x[:, tile, :], in0=ps[:, :], scalar=cw[:, tile, e - 1:e],
                            in1=x[:, tile, :], op0=ALU.mult, op1=ALU.add))
                    x_ready[tile] = t
                    down.release(dj, t)
                zs_ring.release(zj, pe.last())
                if h == 1:
                    wf_ring.release(j, pe.last())

            def top(src, mx_, idx, idxf, onehot, k, n_exp, t):
                dve.wait(t)
                for b in range(B):
                    t = dve.did(nc.vector.max(mx_[:, b, :], src[:, b, :]))
                dve.wait(t)
                for b in range(B):
                    t = dve.did(nc.vector.max_index(idx[:, b, :], mx_[:, b, :], src[:, b, :]))
                dve.wait(t)
                t = dve.did(nc.vector.tensor_copy(idxf[:, :, :], idx[:, :, 0:k]))
                dve.wait(t, t_const)
                return dve.did(nc.vector.tensor_tensor(
                    onehot[:, :, :, :], idxf[:, :, :].unsqueeze(3).broadcast_to([P, B, k, n_exp]),
                    iota[:, 0:n_exp].unsqueeze(1).unsqueeze(1).broadcast_to([P, B, k, n_exp]), ALU.is_equal))

            gj, gps, free = down.take()
            pe.wait(free, t_g, t_xn[1])
            for b in range(B):
                h, cols = b // HB, slice((b % HB) * P, (b % HB + 1) * P)
                t = mm_group(gps[:, b * E0:(b + 1) * E0], [q for k in range(KT) for q in three(
                    (xnT[h][0][:, k, cols], xnT[h][1][:, k, cols]), (gate[0][:, k, :], gate[1][:, k, :]))])
            act.wait(t)
            t = act.did(nc.scalar.activation(sc[:, :, :], gps[:, 0:B * E0].rearrange("p (b e) -> p b e", b=B),
                                             ACT.Sigmoid))
            down.release(gj, t)
            dve.wait(t, t_gb)
            t = dve.did(nc.vector.tensor_tensor(
                sc[:, :, :], sc[:, :, :], gbias[:, :].unsqueeze(1).broadcast_to([P, B, E0]), ALU.add))
            t = top(sc, mx, mi_, mif, oh, TOP0, E0, t)
            dve.wait(t)
            t = dve.did(nc.vector.tensor_reduce(cw[:, :, :], oh[:, :, :, :].rearrange("p b k e -> p b e k"),
                                                AX.X, ALU.add))
            dve.wait(t)
            t = dve.did(nc.vector.tensor_tensor(cw[:, :, :], cw[:, :, :], sc[:, :, :], ALU.mult))
            t2 = dve.did(nc.vector.tensor_reduce(ssum[:, :], mx[:, :, 0:TOP0], AX.X, ALU.add))
            dve.wait(t2)
            t2 = dve.did(nc.vector.tensor_scalar(ssum[:, :], ssum[:, :], 1e-20, None, ALU.add))
            dve.wait(t2)
            t2 = dve.did(nc.vector.reciprocal(ssum[:, :], ssum[:, :]))
            dve.wait(t2)
            t_cw = dve.did(nc.vector.tensor_tensor(
                cw[:, :, :], cw[:, :, :], ssum[:, :].unsqueeze(2).broadcast_to([P, B, E0]), ALU.mult))

            before = None
            for e in experts:
                for h in range(2):
                    z_ = hidden(e, h)
                    if before:
                        output(*before)
                    before = (e, h, *z_)
                    if h == 0:
                        if e + 1 <= E0:
                            queue_split(e + 1)
                        background(3)
                    else:
                        background(6)
            output(*before)
            fence()
            scope.pop()

        with ExitStack() as phase:
            scope.append(phase)
            kT = pair("k1T", [P, KV1, 2, HT])
            v = pair("v1", [P, 2, HB, D])
            head = [pair(f"w1q{i}", [P, KT, P]) for i in range(4)]
            outw = [pair(f"w1o{i}", [P, D]) for i in range(2 * UH)]
            raw = [sb(f"w1_raw{i}", [P, D]) for i in range(3)]
            qT = [pair(f"q1T{i}", [P, UH, HT]) for i in range(2)]
            pr = [sb(f"p1_{i}", [P, UH, 2 * P]) for i in range(2)]
            pT = pair("p1T", [P, 2, UH * P])
            aT = pair("a1T", [P, UH * P])
            mx = [sb(f"mx1_{i}", [P, 4 * UH]) for i in range(4)]

            land = Landing(raw, [sem(f"ld_w1{i}") for i in range(3)])
            head_ring, out_ring = Ring(head), Ring(outw)
            s_ring = Ring(bank[0:4])
            t_ring, o_ring, y_ring = Ring(bank[4:5]), Ring(bank[5:6]), Ring(bank[6:8])
            pr_ring = Ring(pr)
            q_free = [None, None]
            pT_free = [None, None]
            aT_free = None
            xn_free = None
            kv_free = None

            def step_weights(u, b):
                n = UH * u + b + UH + 2
                w = [("wq1", n, head_ring)] if n < H1 else []
                if b >= 2 and u + 1 < UNITS:
                    w += [("wo1", UH * (u + 1) + 2 * (b - 2) + h, out_ring) for h in range(2)]
                return w

            stream = []
            for half in range(2):
                stream += [("wk1", g, head_ring) for g in range(KV1)]
                stream += [("wv1", k, out_ring) for k in range(KT)]
                stream += [("wq1", h, head_ring) for h in range(UH)]
                stream += [("wo1", h, out_ring) for h in range(UH)]
                stream += [("wq1", UH + n, head_ring) for n in range(2)]
                for u in range(UNITS):
                    for b in range(HB):
                        stream += step_weights(u, b)
            loads, splits = list(stream), []
            have = {"head": [], "out": []}

            def fetch():
                if loads:
                    name, n, ring = loads.pop(0)
                    i, buf, free = land.take()
                    sp.wait(free)
                    t = land.filled(i, nc.sync.dma_start(buf[:, :], A[name][n]))
                    splits.append((ring, i, buf, t))

            def weight():
                if not splits:
                    return
                ring, i, buf, t_in = splits.pop(0)
                j, dst, free = ring.take()
                if ring is head_ring:
                    hi, lo = (q[:, :, :].rearrange("p k c -> p (k c)") for q in dst)
                else:
                    hi, lo = (q[:, :] for q in dst)
                t = split(hi, lo, buf[:, :], [t_in], free)
                land.release(i, t)
                have["head" if ring is head_ring else "out"].append((j, dst, t))
                fetch()

            for _ in raw:
                fetch()

            def project(w, t_w_, src, t_src, dst, dst_free, ring=s_ring):
                sj, ps, free = ring.take()
                pe.wait(free, t_w_, *t_src)
                t = mm_group(ps[:, :], [q for k in range(KT) for q in three(
                    (w[0][:, k, :], w[1][:, k, :]), (src[0][:, k, :], src[1][:, k, :]))])
                t2 = split(dst[0], dst[1], ps[:, :], [t], dst_free)
                ring.release(sj, t2)
                return t, t2

            s_ctx = [sem(f"ld_ctx1{i}") for i in range(2)]
            n_ctx = [0, 0]
            for half in range(2):
                ctxT = qT[1]
                for k in range(KT):
                    xj, xbuf, xfree = xn_ring.take()
                    sp.wait(xfree)
                    nc.sync.dma_start(xbuf[:, :], A["ctxT"][half][:, k, :]).then_inc(s_ctx[xj], 16)
                    n_ctx[xj] += 16
                    t_c = split(ctxT[0][:, k, :], ctxT[1][:, k, :], xbuf[:, :], [(s_ctx[xj], n_ctx[xj])], q_free[1])
                    xn_ring.release(xj, t_c)
                for _ in range(KV1):
                    weight()
                wk = have["head"]
                have["head"] = []
                for g in range(KV1):
                    _, t_kc = project(wk[g][1], wk[g][2], ctxT, [t_c],
                                      (kT[0][:, g, 0, :], kT[1][:, g, 0, :]), kv_free)
                for _ in range(KT):
                    weight()
                wv = have["out"]
                have["out"] = []

                def value_tiles(part, src, t_src):
                    for b in range(HB):
                        cols = slice(b * P, (b + 1) * P)
                        sj, ps, free = s_ring.take()
                        pe.wait(free, *t_src, *[w[2] for w in wv])
                        t = mm_group(ps[:, :], [q for k in range(KT) for q in three(
                            (src[0][:, k, cols], src[1][:, k, cols]), (wv[k][1][0][:, :], wv[k][1][1][:, :]))])
                        t2 = split(v[0][:, part, b, :], v[1][:, part, b, :], ps[:, :], [t], kv_free)
                        s_ring.release(sj, t2)
                    return t, t2

                t_cfree, _ = value_tiles(0, ctxT, [t_c])
                q_free[1] = t_cfree
                t_xn = layer_norm(range(half * HB, half * HB + HB), xnA, y_ring, xn_free)
                for g in range(KV1):
                    t, t_kx = project(wk[g][1], wk[g][2], xnA, [t_xn],
                                      (kT[0][:, g, 1, :], kT[1][:, g, 1, :]), kv_free)
                    head_ring.release(wk[g][0], t)
                t, t_kv = value_tiles(1, xnA, [t_xn])
                for k in range(KT):
                    out_ring.release(wv[k][0], t)

                steps = [(u, b) for u in range(UNITS) for b in range(HB)]
                state, t_qs = {}, {}

                def query(n):
                    nonlocal xn_free
                    u, h = divmod(n, UH)
                    j, w, t_w_ = have["head"].pop(0)
                    dst = qT[u % 2]
                    t, t2 = project(w, t_w_, xnA, [t_xn], (dst[0][:, h, :], dst[1][:, h, :]), q_free[u % 2],
                                    y_ring)
                    head_ring.release(j, t)
                    xn_free = t
                    if h == UH - 1:
                        t_qs[u] = t2

                def scores(i):
                    u, b = steps[i]
                    g = u * UH // (H1 // KV1)
                    tok = slice(b * P, (b + 1) * P)
                    q = qT[u % 2]
                    st = state[i] = {"s": []}
                    for pr_ in range(UH // 2):
                        sj, ps, free = s_ring.take()
                        pe.wait(free, t_qs[u], t_kv)
                        for hh in range(2):
                            h = 2 * pr_ + hh
                            t = mm_group(ps[:, hh * 2 * P:(hh + 1) * 2 * P], three(
                                (q[0][:, h, tok], q[1][:, h, tok]),
                                (kT[0][:, g, :, tok], kT[1][:, g, :, tok])))
                        st["s"].append((sj, ps, t))
                    if b == HB - 1:
                        q_free[u % 2] = t

                def softmax_max(i):
                    st = state[i]
                    m = mx[i % 4]
                    for n, (_, ps, t) in enumerate(st["s"]):
                        dve.wait(t)
                        t = dve.did(nc.vector.tensor_reduce(
                            m[:, 2 * n:2 * n + 2], ps[:, :].rearrange("p (h k) -> p h k", h=2), AX.X, ALU.max))
                    dve.wait(t)
                    st["nb"] = dve.did(nc.vector.tensor_scalar(m[:, UH:2 * UH], m[:, 0:UH], -SCALE1, None, ALU.mult))

                def softmax_exp(i):
                    st = state[i]
                    st["j"], _, free = pr_ring.take()
                    j, m = st["j"], mx[i % 4]
                    act.wait(st["nb"], free)
                    for n, (sj, ps, _) in enumerate(st["s"]):
                        for hh in range(2):
                            h = 2 * n + hh
                            t = act.did(nc.scalar.activation(
                                pr[j][:, h, :], ps[:, hh * 2 * P:(hh + 1) * 2 * P], ACT.Exp,
                                bias=m[:, UH + h:UH + h + 1], scale=SCALE1,
                                accum_out=m[:, 2 * UH + h:2 * UH + h + 1]))
                        s_ring.release(sj, t)
                    st["e"] = t

                def softmax_norm(i):
                    st = state[i]
                    j, m = st["j"], mx[i % 4]
                    dve.wait(st["e"])
                    t = dve.did(nc.vector.reciprocal(m[:, 3 * UH:4 * UH], m[:, 2 * UH:3 * UH]))
                    pool.wait(t, st["e"])
                    for h in range(UH):
                        t = pool.did(nc.gpsimd.tensor_scalar(
                            pr[j][:, h, :], pr[j][:, h, :], m[:, 3 * UH + h:3 * UH + h + 1],
                            1.0, ALU.mult, ALU.mult))
                    st["p"] = t

                def turn(i, part):
                    st = state[i]
                    tj, ps, free = t_ring.take()
                    pe.wait(free, st["p"], t_const)
                    for h in range(UH):
                        ins = nc.tensor.transpose(ps[:, h * P:(h + 1) * P],
                                                  pr[st["j"]][:, h, part * P:(part + 1) * P], ident)
                    t = pe.did(ins)
                    t2 = split(pT[0][:, part, :], pT[1][:, part, :], ps[:, :], [t], pT_free[part])
                    t_ring.release(tj, t2)
                    st.setdefault("pT", []).append(t2)
                    if part == 1:
                        pr_ring.release(st["j"], t)

                def attend(i):
                    nonlocal aT_free
                    st = state[i]
                    u, b = steps[i]
                    g = u * UH // (H1 // KV1)
                    oj, ps, free = o_ring.take()
                    pe.wait(free)
                    prs = []
                    for part in range(2):
                        vv = tuple(q[:, part, b, g * P:(g + 1) * P] for q in v)
                        prs += three(vv, (pT[0][:, part, :], pT[1][:, part, :]))
                    for n, (a, c) in enumerate(prs):
                        pe.wait(st["pT"][n // 3])
                        ins = nc.tensor.matmul(ps[:, :], a, c, start=(n == 0), stop=(n == 5))
                        if n % 3 == 2:
                            t = pT_free[n // 3] = pe.did(ins)
                    t2 = split(aT[0][:, :], aT[1][:, :], ps[:, :], [t], aT_free)
                    o_ring.release(oj, t2)
                    st["a"] = t2

                def project_out(i):
                    nonlocal aT_free
                    st = state.pop(i)
                    u, b = steps[i]
                    if b == 0:
                        wos[u] = [have["out"].pop(0) for _ in range(UH)]
                    ws = wos[u]
                    yj, ps, free = y_ring.take()
                    pe.wait(free, st["a"], *[w[2] for w in ws])
                    t = mm_group(ps[:, :], [q for h in range(UH) for q in three(
                        (aT[0][:, h * P:(h + 1) * P], aT[1][:, h * P:(h + 1) * P]),
                        (ws[h][1][0][:, :], ws[h][1][1][:, :]))])
                    aT_free = t
                    if b == HB - 1:
                        for w in ws:
                            out_ring.release(w[0], t)
                    tile = half * HB + b
                    dve.wait(t, x_ready[tile])
                    t = dve.did(nc.vector.tensor_tensor(x[:, tile, :], ps[:, :], x[:, tile, :], ALU.add))
                    x_ready[tile] = t
                    y_ring.release(yj, t)

                wos = {}
                for h in range(2 * UH):
                    weight()
                for n in range(UH):
                    query(n)
                weight()
                weight()
                query(UH)
                n_steps = len(steps)
                for i in range(-1, n_steps + 2):
                    u, b = steps[i] if 0 <= i < n_steps else (UNITS, 0)
                    if i + 1 < n_steps:
                        scores(i + 1)
                        softmax_max(i + 1)
                    if 1 <= i <= n_steps:
                        turn(i - 1, 0)
                    if 0 <= i < n_steps and i + UH + 1 < H1:
                        query(i + UH + 1)
                    if 1 <= i <= n_steps:
                        turn(i - 1, 1)
                    if i + 1 < n_steps:
                        softmax_exp(i + 1)
                    if i >= 2:
                        project_out(i - 2)
                    if i + 1 < n_steps:
                        softmax_norm(i + 1)
                    if 0 <= i < n_steps:
                        for _ in step_weights(u, b):
                            weight()
                    if 1 <= i <= n_steps:
                        attend(i - 1)
                kv_free = pe.last()
            fence()
            scope.pop()

        with ExitStack() as phase:
            scope.append(phase)
            xnB = pair("xnB2", [P, KT, HT])
            xnT = [xnA, xnB]
            wm_raw, wm = sb("wm_raw", [P, KT, D]), pair("wm", [P, KT, D])
            ws_raw, ws = sb("ws_raw", [P, KT, SMALL]), pair("ws", [P, KT, SMALL])
            lb_raw, lb = sb("lb_raw", [P, D]), pair("lb", [P, D])
            vecs = sb("vecs", [P, 3 * G1 + E1])
            gw2 = sb("gw2", [P, E1, G1])
            h_ = sb("h_", [P, B, G1])
            hc = sb("hc", [P, B, G1])
            prod = sb("prod", [P, B, E1, G1])
            tmp = sb("tmp", [P, B, P])
            st1 = sb("st1", [P, B])
            st2 = sb("st2", [P, B])
            gates = sb("gates", [P, B, E1])
            mx = sb("mxg", [P, B, 8])
            mi_ = sb("mig", [P, B, 8], U32)
            mif = sb("migf", [P, B, TOP1])
            oh = sb("ohg", [P, B, TOP1, E1])
            gk = sb("gk", [P, B, TOP1])
            allowed = sb("allowed", [P, TOP1, E1])
            w1 = sb("w1g", [P, B, E1])
            lo_a = [pair(f"loa{i}", [P, P]) for i in range(2)]

            ones = sb("ones", [P, P])[:, :]
            t_m = loaded("wm", wm_raw[:, :, :], A["wm1"])
            t_s = loaded("ws", ws_raw[:, :, :], A["ws1"])
            t_l = loaded("lb", lb_raw[:, :], A["lb1"])
            t_vec = loaded("vecs", vecs[:, :], A["vecs1"].broadcast_to([P, 3 * G1 + E1]))
            t_gw2 = loaded("gw2", gw2[:, :, :], A["gw2"].broadcast_to([P, E1, G1]))
            for k in range(KT):
                t_ws = split(ws[0][:, k, :], ws[1][:, k, :], ws_raw[:, k, :], [t_s])
            lo_ring = Ring(bank[0:2])
            t_xn = [layer_norm(range(h * HB, h * HB + HB), xnT[h], lo_ring) for h in range(2)]
            for k in range(KT):
                t_wm = split(wm[0][:, k, :], wm[1][:, k, :], wm_raw[:, k, :], [t_m])
            t_lb = split(lb[0][:, :], lb[1][:, :], lb_raw[:, :], [t_l])

            small_banks = bank[2:5]
            t_small = []
            for b in range(B):
                h, cols = b // HB, slice((b % HB) * P, (b % HB + 1) * P)
                ps = small_banks[b // 3][:, (b % 3) * SMALL:(b % 3 + 1) * SMALL]
                pe.wait(t_xn[h], t_ws)
                t_small.append(mm_group(ps, [q for k in range(KT) for q in three(
                    (xnT[h][0][:, k, cols], xnT[h][1][:, k, cols]), (ws[0][:, k, :], ws[1][:, k, :]))]))
            for n in range(3):
                tiles = list(range(3 * n, min(3 * n + 3, B)))
                k = len(tiles)
                src = small_banks[n][:, 0:k * SMALL].rearrange("p (b c) -> p b c", b=k)
                bs = slice(tiles[0], tiles[0] + k)
                dve.wait(t_small[tiles[-1]], t_vec)
                t_h = dve.did(nc.vector.tensor_tensor(
                    h_[:, bs, :], src[:, :, P:SMALL],
                    vecs[:, 0:G1].unsqueeze(1).broadcast_to([P, k, G1]), ALU.add))
                act.wait(t_h)
                t_tmp = act.did(nc.scalar.activation(tmp[:, bs, :], src[:, :, 0:P], ACT.Copy))

            main_ring = Ring(bank[5:8])

            def dense(b):
                h, cols = b // HB, slice((b % HB) * P, (b % HB + 1) * P)
                mj, ps, free = main_ring.take()
                pe.wait(free, t_wm)
                t = mm_group(ps[:, :], [q for k in range(KT) for q in three(
                    (xnT[h][0][:, k, cols], xnT[h][1][:, k, cols]), (wm[0][:, k, :], wm[1][:, k, :]))])
                dve.wait(t, x_ready[b])
                x_ready[b] = dve.did(nc.vector.tensor_tensor(x[:, b, :], ps[:, :], x[:, b, :], ALU.add))
                main_ring.release(mj, x_ready[b])

            dense_left = list(range(B))
            routed = [0]

            def bc(ap, n):
                return ap.unsqueeze(2).broadcast_to([P, B, n])

            def bv_(k0, n):
                return vecs[:, k0:k0 + n].unsqueeze(1).broadcast_to([P, B, n])

            def v_(ins):
                t = dve.did(ins)
                routed[0] += 1
                if dense_left and routed[0] % 3 == 0:
                    dense(dense_left.pop(0))
                dve.wait(t)
                return t

            TT, TS = nc.vector.tensor_tensor, nc.vector.tensor_scalar
            dve.wait(t_h)
            v_(nc.vector.tensor_reduce(st1[:, :], h_[:, :, :], AX.X, ALU.add))
            v_(TS(st1[:, :], st1[:, :], 1.0 / G1, None, ALU.mult))
            v_(TT(h_[:, :, :], h_[:, :, :], bc(st1[:, :], G1), ALU.subtract))
            v_(TT(hc[:, :, :], h_[:, :, :], h_[:, :, :], ALU.mult))
            t = v_(nc.vector.tensor_reduce(st2[:, :], hc[:, :, :], AX.X, ALU.add))
            act.wait(t)
            t = act.did(nc.scalar.activation(st2[:, :], st2[:, :], ACT.Sqrt, bias=eps, scale=1.0 / G1))
            dve.wait(t)
            v_(nc.vector.reciprocal(st2[:, :], st2[:, :]))
            v_(TT(h_[:, :, :], h_[:, :, :], bc(st2[:, :], G1), ALU.mult))
            v_(TT(h_[:, :, :], h_[:, :, :], bv_(G1, G1), ALU.mult))
            v_(TT(h_[:, :, :], h_[:, :, :], bv_(2 * G1, G1), ALU.add))
            v_(TS(h_[:, :, :], h_[:, :, :], 0.0, None, ALU.max))
            dve.wait(t_gw2)
            v_(TT(prod[:, :, :, :], h_[:, :, :].unsqueeze(2).broadcast_to([P, B, E1, G1]),
                  gw2[:, :, :].unsqueeze(1).broadcast_to([P, B, E1, G1]), ALU.mult))
            v_(nc.vector.tensor_reduce(gates[:, :, :], prod[:, :, :, :], AX.X, ALU.add))
            t = v_(TT(gates[:, :, :], gates[:, :, :], bv_(3 * G1, E1), ALU.add))
            t_oh = top(gates, mx, mi_, mif, oh, TOP1, E1, t)
            v_(TT(gk[:, :, :], mx[:, :, 0:TOP1], mx[:, :, 0:1].broadcast_to([P, B, TOP1]), ALU.subtract))
            act.wait(dve.last())
            t = act.did(nc.scalar.activation(gk[:, :, :], gk[:, :, :], ACT.Exp))
            cps = bank[0]
            t_ones = pool.did(nc.gpsimd.memset(ones, 1.0))
            pe.wait(t_ones)
            pe.wait(t_oh, lo_ring.reader[0], t_const)
            t_cnt = mm_group(cps[:, 0:TOP1 * E1], [(ones, oh[:, b, :, :].rearrange("p k e -> p (k e)"))
                                                   for b in range(B)])
            dve.wait(t_cnt)
            v_(TS(allowed[:, :, :], cps[:, 0:TOP1 * E1].rearrange("p (k e) -> p k e", k=TOP1),
                  float(CAPACITY), 1.0 / R1, ALU.is_le, ALU.mult))
            dve.wait(t)
            v_(nc.vector.tensor_reduce(st1[:, :], gk[:, :, :], AX.X, ALU.add))
            v_(nc.vector.reciprocal(st1[:, :], st1[:, :]))
            v_(TT(gk[:, :, :], gk[:, :, :], bc(st1[:, :], TOP1), ALU.mult))
            for k in range(TOP1):
                v_(TT(oh[:, :, k, :], oh[:, :, k, :], bc(gk[:, :, k], E1), ALU.mult))
                v_(TT(oh[:, :, k, :], oh[:, :, k, :],
                      allowed[:, k, :].unsqueeze(1).broadcast_to([P, B, E1]), ALU.mult))
            v_(TT(w1[:, :, :], oh[:, :, 0, :], oh[:, :, 1, :], ALU.add))
            dve.wait(t_tmp)
            t4 = tmp[:, :, :].rearrange("p b (e r) -> p b e r", e=E1)
            t_w1 = v_(TT(t4, t4, w1[:, :, :].unsqueeze(3).broadcast_to([P, B, E1, R1]), ALU.mult))
            while dense_left:
                dense(dense_left.pop(0))
            turn_ring, lora_ring, la_ring = Ring(bank[0:2]), Ring(bank[2:5]), Ring(lo_a)
            turn_ring.release(0, t_w1)
            s_out = sem("stored")
            for b in range(B):
                tj, ps, free = turn_ring.take()
                pe.wait(free, t_w1)
                t = pe.did(nc.tensor.transpose(ps[:, 0:P], tmp[:, b, :], ident))
                aj, abuf, afree = la_ring.take()
                t = split(abuf[0][:, :], abuf[1][:, :], ps[:, 0:P], [t], afree)
                turn_ring.release(tj, t)
                rj, ps, free = lora_ring.take()
                pe.wait(free, t, t_lb)
                t = mm_group(ps[:, :], three((abuf[0][:, :], abuf[1][:, :]), (lb[0][:, :], lb[1][:, :])))
                la_ring.release(aj, t)
                dve.wait(t, x_ready[b])
                t = dve.did(nc.vector.tensor_tensor(x[:, b, :], ps[:, :], x[:, b, :], ALU.add))
                lora_ring.release(rj, t)
                sp.wait(t)
                nc.sync.dma_start(out[b], x[:, b, :]).then_inc(s_out, 16)
            nc.sync.wait_ge(s_out, 16 * B)
            scope.pop()


def constants():
    import numpy as np

    c = np.zeros((P, CONST), np.float32)
    c[:, C_ID:C_ID + P] = np.eye(P)
    for p in range(P):
        c[p, C_MASK + (p // HD0) % G0] = 1.0
    c[:, C_IOTA:C_IOTA + 16] = np.arange(16)
    c[:, C_EPS] = LN_EPS
    return c


def selectors():
    import numpy as np

    s = np.zeros((P, KT, P), np.float32)
    for m in range(KT):
        for col in range(P):
            j, d = col // (G0 * HD0), col % HD0
            s[(2 * m + j) * HD0 + d, m, col] = 1.0
    return s


def layout(i):
    import numpy as np

    def rows(w):
        return w.reshape(w.shape[0] // P, P, w.shape[1]).transpose(1, 0, 2)

    def row(v):
        return v.reshape(1, -1)

    a = {k: np.asarray(v) for k, v in i.items()}
    wffn = np.stack([
        np.stack([rows(w.T).reshape(P, 2, 512) for w in (g, u, d)], axis=1)
        for g, u, d in [(a["L0_ffn_Sg"], a["L0_ffn_Su"], a["L0_ffn_Sd"]),
                        *zip(a["L0_ffn_Wg"], a["L0_ffn_Wu"], a["L0_ffn_Wd"])]])
    by_head = lambda w: rows(w).reshape(P, KT, w.shape[1] // P, P).transpose(2, 0, 1, 3).reshape(-1, P, D)
    lora_a = a["L1_ffn_lora_A"].transpose(1, 0, 2).reshape(D, E1 * R1)
    laid = {
        "consts": constants(),
        "sel": selectors(),
        "x": a["x"],
        "ctxT": rows(a["ctx_4096"].reshape(B * P, D).T).reshape(P, KT, 2, HT).transpose(2, 0, 1, 3),
        "wq0": rows(a["L0_xattn_Wq"]),
        "wkv0": np.stack([rows(a["L0_xattn_Wk"]), rows(a["L0_xattn_Wv"])], axis=1),
        "wo0": a["L0_xattn_Wo"].reshape(KV0, G0, HD0, D).transpose(0, 2, 1, 3).reshape(P, G0, D),
        "bq0": a["L0_xattn_bq"].reshape(KT, P).T,
        "bk0": a["L0_xattn_bk"].reshape(P, 1),
        "bv0": row(a["L0_xattn_bv"]),
        "bo0": row(a["L0_xattn_bo"]),
        "gate0": rows(a["L0_ffn_gate_w"].T),
        "gbias0": row(a["L0_ffn_bias"]),
        "wffn": wffn,
        "wk1": by_head(a["L1_xattn_Wk"]),
        "wv1": a["L1_xattn_Wv"].reshape(KT, P, D),
        "wq1": by_head(a["L1_xattn_Wq"]),
        "wo1": a["L1_xattn_Wo"].reshape(H1, P, D),
        "wm1": rows(a["L1_ffn_weight"].T),
        "ws1": rows(np.concatenate([lora_a, a["L1_ffn_gw1"].T], axis=1)),
        "lb1": a["L1_ffn_lora_B"].reshape(E1 * R1, D),
        "vecs1": row(np.concatenate([a["L1_ffn_gb1"], a["L1_ffn_ln_gamma"], a["L1_ffn_ln_beta"], a["L1_ffn_gb2"]])),
        "gw2": a["L1_ffn_gw2"].reshape(1, E1, G1),
    }
    return {k: np.ascontiguousarray(v) for k, v in laid.items()}


def kernel(**inputs):
    import concourse.bacc as bacc
    from concourse.bass_utils import run_bass_kernel_spmd

    laid = layout(inputs)
    nc = bacc.Bacc("TRN2", target_bir_lowering=False, num_devices=1)
    A = {name: nc.dram_tensor("in_" + name, a.shape, mybir.dt.from_np(a.dtype), kind="ExternalInput").ap()
         for name, a in laid.items()}
    out = nc.dram_tensor("out", (B, P, D), F32, kind="ExternalOutput").ap()
    layers_kernel(nc, A, out)
    r = run_bass_kernel_spmd(nc, [{"in_" + name: a for name, a in laid.items()}], core_ids=[0])
    return r.results[0]["out"]
```

```python
from contextlib import ExitStack
from itertools import chain

import concourse.bass as bass
from concourse import mybir

F32 = mybir.dt.float32
F32R = mybir.dt.float32r
U32 = mybir.dt.uint32
ALU = mybir.AluOpType
ACT = mybir.ActivationFunctionType
AX = mybir.AxisListType

P = 128
B = 8
D = 512
KT = D // P
HB = B // 2
HT = HB * P
LN_EPS = 1e-5

H0, KV0, HD0 = 32, 8, 16
G0 = H0 // KV0
E0, TOP0, I0 = 16, 4, 256
IT = I0 // P
H1, KV1 = 32, 4
UH = 4
UNITS = H1 // UH
SCALE0 = float(HD0) ** -0.5
SCALE1 = float(P) ** -0.5
E1, TOP1, R1 = 8, 2, 16
G1 = 4 * E1
SMALL = P + G1
CAPACITY = int(3.0 * B * P / E1)

C_ID, C_MASK, C_IOTA, C_EPS = 0, 128, 132, 148
CONST = 149


class Queue:

    def __init__(self, eng, sem):
        self.eng, self.sem, self.count, self.seen = eng, sem, 0, {}

    def wait(self, *tokens):
        for t in tokens:
            if t is None:
                continue
            if isinstance(t, list):
                self.wait(*t)
                continue
            sem, value = t
            if self.seen.get(sem.name, 0) < value:
                self.eng.wait_ge(sem, value)
                self.seen[sem.name] = value

    def did(self, ins):
        self.count += 1
        ins.then_inc(self.sem, 1)
        return (self.sem, self.count)

    def last(self):
        return (self.sem, self.count)


class Ring:

    def __init__(self, bufs):
        self.bufs, self.reader, self.at = bufs, [None] * len(bufs), 0
        self.taken = [False] * len(bufs)

    def take(self):
        i = self.at % len(self.bufs)
        self.at += 1
        assert not self.taken[i], "taken before its last reader is known"
        self.taken[i] = True
        return i, self.bufs[i], self.reader[i]

    def release(self, i, token):
        self.reader[i], self.taken[i] = token, False


class Landing(Ring):

    def __init__(self, bufs, sems):
        super().__init__(bufs)
        self.sems, self.fills = sems, [0] * len(bufs)

    def filled(self, i, ins):
        self.fills[i] += 1
        ins.then_inc(self.sems[i], 16)
        return (self.sems[i], 16 * self.fills[i])


def three(hi_lo_a, hi_lo_b):
    (ah, al), (bh, bl) = hi_lo_a, hi_lo_b
    return (ah, bh), (ah, bl), (al, bh)


def layers_kernel(nc, A, out):
    with ExitStack() as whole:
        base = (nc.sbuf_base + 31) // 32 * 32
        place = [base]

        def sb(name, shape, dt=F32):
            n = 4
            for k in shape[1:]:
                n *= k
            t = nc.alloc_sbuf_tensor_at(name, shape, dt, offset=place[0])
            place[0] += (n + 31) // 32 * 32
            assert place[0] <= nc.sbuf_usable_end, (name, place[0] - nc.sbuf_usable_end)
            return t

        def pair(name, shape):
            return sb(name + "_hi", shape, F32R), sb(name + "_lo", shape, F32R)

        def sem(name):
            return whole.enter_context(nc.semaphore(name))

        pe = Queue(nc.tensor, sem("pe_done"))
        act = Queue(nc.scalar, sem("act_done"))
        dve = Queue(nc.vector, sem("dve_done"))
        pool = Queue(nc.gpsimd, sem("pool_done"))
        sp = Queue(nc.sync, None)

        def load(dst, src, sem_):
            nc.sync.dma_start(dst, src).then_inc(sem_, 16)
            return (sem_, 16)

        def loaded(name, dst, src):
            return load(dst, src, sem("ld_" + name))

        def split(hi, lo, src, ready, free=None, lo_on=None):
            act.wait(*ready, free)
            t = act.did(nc.scalar.activation(hi, src, ACT.Copy))
            q = lo_on or dve
            q.wait(t, *ready, free)
            return q.did(q.eng.tensor_tensor(lo, src, hi.bitcast(F32), ALU.subtract))

        def mm_group(dst, pairs, mark=True):
            pairs = list(pairs)
            for n, (a, b) in enumerate(pairs):
                ins = nc.tensor.matmul(dst, a, b, start=(n == 0), stop=(n == len(pairs) - 1))
            return pe.did(ins) if mark else None

        def now():
            return [q.last() for q in (pe, act, dve, pool) if q.count]

        bank = [whole.enter_context(nc.psum_tensor(f"bank{i}", [P, 512], F32)) for i in range(8)]

        x = sb("x", [P, B, D])
        x_ready = [None] * B
        xnA = pair("xnA", [P, KT, HT])
        consts = sb("consts", [P, CONST])
        ident = consts[:, C_ID:C_ID + P]
        eps = consts[:, C_EPS:C_EPS + 1]
        iota = consts[:, C_IOTA:C_IOTA + 16]
        stats = sb("stats", [P, B, 6])
        moments = sb("moments", [P, B, 2])
        rstd = sb("rstd", [P, B])
        xn = [sb(f"xn{i}", [P, D]) for i in range(2)]
        xn_ring = Ring(xn)

        PHASE = place[0]
        t_const = loaded("consts", consts[:, :], A["consts"])
        s_x = [sem(f"ld_x{b}") for b in range(B)]

        def norm_pieces(tiles, dest, banks, dest_free, said):
            b0, n = tiles[0], len(tiles)
            for b in tiles:
                dve.wait(x_ready[b])
                t = dve.did(nc.vector.bn_stats(stats[:, b, :], x[:, b, :]))
                dve.wait(t)
                t = dve.did(nc.vector.bn_aggr(moments[:, b, :], stats[:, b, :]))
                if b % 2 == 1 and b != tiles[-1]:
                    yield
            act.wait(t, t_const)
            r = rstd[:, b0:b0 + n]
            t = act.did(nc.scalar.activation(r, moments[:, b0:b0 + n, 1], ACT.Sqrt, bias=eps))
            yield
            dve.wait(t)
            t_r = dve.did(nc.vector.reciprocal(r, r))
            dve.wait(t_r)
            ahead = {}
            for k in range(n + 1):
                if k < n:
                    b = tiles[k]
                    i, buf, free = xn_ring.take()
                    dve.wait(free)
                    t = dve.did(nc.vector.tensor_scalar(buf[:, :], x[:, b, :], moments[:, b, 0:1],
                                                        rstd[:, b:b + 1], ALU.subtract, ALU.mult))
                    ahead[k] = (i, buf, t)
                if k >= 1:
                    b = tiles[k - 1]
                    i, buf, t = ahead.pop(k - 1)
                    j, ps, ps_free = banks.take()
                    pe.wait(t, t_const, ps_free)
                    for c in range(KT):
                        ins = nc.tensor.transpose(ps[:, c * P:(c + 1) * P], buf[:, c * P:(c + 1) * P], ident)
                    t = pe.did(ins)
                    xn_ring.release(i, t)
                    cols = slice((b % HB) * P, (b % HB + 1) * P)
                    ps3 = ps[:, :].rearrange("p (k t) -> p k t", k=KT)
                    said["t"] = split(dest[0][:, :, cols], dest[1][:, :, cols], ps3, [t], dest_free and dest_free())
                    banks.release(j, said["t"])
                yield

        def run(pieces, n=None):
            while n is None or n > 0:
                if next(pieces, False) is False:
                    break
                n = n and n - 1

        place[0] = PHASE
        ctxT = pair("ctx0", [P, KT, HT])
        first_raw = place[0]
        ctxT_raw = sb("ctx0_raw", [P, KT, HT])
        w_raw = sb("w0_raw", [P, KT, D])
        place[0] = first_raw
        qT = [None, pair("q0T1", [P, KT, HT])]
        wq = pair("wq0", [P, KT, D])
        wkv = pair("wkv0", [P, 2, KT, P])
        qT[0] = pair("q0T0", [P, KT, HT])
        kT = pair("k0T", [P, HT])
        v = sb("v0", [P, HB, P])
        kd = [pair(f"k0d{i}", [P, KT, G0, P]) for i in range(2)]
        sel = sb("sel", [P, KT, P], F32R)
        wo = pair("wo0", [P, KT, D])
        vp = [pair(f"v0p{i}", [P, KV0, P]) for i in range(2)]
        bq = sb("bq0", [P, KT])
        bk = sb("bk0", [P, 1])
        bv = sb("bv0", [P, P])
        bo = sb("bo0", [P, D])
        PR, SX = 4, 6
        pr = sb("p0", [P, PR, G0, P])
        sx = sb("sx0", [P, SX, 4, G0])
        pT = [pair(f"p0T{i}", [P, HT]) for i in range(2)]
        krep = pair("k0rep", [P, KT, P])
        aT = pair("a0T", [P, G0 * P])

        small_raw = pr[:, 0:2, :, :]
        sel_raw = pr[:, 2, :, :]
        mask = consts[:, C_MASK:C_MASK + G0]
        s_ctx = [sem(f"ld_ctx0{part}") for part in range(2)]

        t_kv = [loaded("wk0", small_raw[:, 0], A["wkv0"][:, 0])]
        t_ctx = []
        for part in range(2):
            ks = slice(part * KT // 2, (part + 1) * KT // 2)
            nc.sync.dma_start(ctxT_raw[:, ks, :], A["ctxT"][0][:, ks, :]).then_inc(s_ctx[part], 16)
            t_ctx.append((s_ctx[part], 16))
        t_kv.append(loaded("wv0", small_raw[:, 1], A["wkv0"][:, 1]))
        t_bk = loaded("bk0", bk[:, :], A["bk0"])
        t_sel_raw = loaded("sel", sel_raw, A["sel"])
        for b in range(HB):
            x_ready[b] = load(x[:, b, :], A["x"][b], s_x[b])
        t_bv = loaded("bv0", bv[:, :], A["bv0"].broadcast_to([P, P]))
        t_wq = loaded("wq0", w_raw[:, :, :], A["wq0"])
        t_bq = loaded("bq0", bq[:, :], A["bq0"])
        t_bo = loaded("bo0", bo[:, :], A["bo0"].broadcast_to([P, D]))
        for b in range(HB, B):
            x_ready[b] = load(x[:, b, :], A["x"][b], s_x[b])

        t_zero = []
        for hi, lo in vp:
            for half_ in (hi, lo):
                t_zero.append(pool.did(nc.gpsimd.memset(half_[:, :, :].bitcast(F32), 0.0)))
        pool.wait(t_sel_raw)
        t_sel = pool.did(nc.gpsimd.tensor_copy(sel[:, :, :], sel_raw))

        banks = Ring(bank[0:4])
        s_ring, t_ring = Ring(bank[0:3]), Ring(bank[3:5])
        o_ring, y_ring = Ring(bank[5:6]), Ring(bank[6:8])

        t_w = {}
        said = {}
        t_w["k"] = split(wkv[0][:, 0], wkv[1][:, 0], small_raw[:, 0], [t_kv[0]])

        def context_pieces(t_in, free):
            for k in range(KT):
                t = split(ctxT[0][:, k, :], ctxT[1][:, k, :], ctxT_raw[:, k, :], [t_in[2 * k // KT]], free)
                said["ctx"] = t
                yield

        def bias_pieces(half):
            for b in range(half * HB, half * HB + HB):
                pool.wait(said["t"], t_bo)
                x_ready[b] = pool.did(nc.gpsimd.tensor_tensor(x[:, b, :], x[:, b, :], bo[:, :], ALU.add))
            yield

        place[0] = PHASE
        xnB = pair("xnB", [P, KT, HT])
        xnT = [xnA, xnB]
        CH = 512
        s_act = [sb(f"silu{i}", [P, HT]) for i in range(2)]
        z = [sb(f"z{i}", [P, HT]) for i in range(2)]
        zs = [pair("zs0", [P, IT, HT])]
        wf = [pair("wf0", [P, 3, 2, CH])]
        raw = [sb("wf_raw0", [P, 3, 2, CH])]
        gate_raw = sb("gate_raw", [P, KT, E0])
        gate = pair("gate", [P, KT, E0])
        gbias = sb("gbias", [P, E0])
        scT = sb("scT", [E0, HT])
        sc = sb("sc", [P, B, E0])
        cw = sb("cw", [P, B, E0])
        zs.append(pair("zs1", [P, IT, HT]))
        raw.append(sb("wf_raw1", [P, 3, 2, CH]))
        wf.append(pair("wf1", [P, 3, 2, CH]))
        above_experts = place[0]
        mx = sb("mxf", [P, B, 8])
        mi_ = sb("mif", [P, B, 8], U32)
        mif = sb("mifl", [P, B, TOP0])
        oh = sb("ohf", [P, B, TOP0, E0])
        ssum = sb("ssum", [P, B])

        land = Landing(raw, [sem(f"ld_wf{i}") for i in range(2)])
        wf_ring = Ring(wf)
        up = Ring(bank[0:4])
        down = Ring(bank[4:8])
        silu_ring, z_ring, zs_ring = Ring(s_act), Ring(z), Ring(zs)

        fetched, ready = {}, {}

        def fetch(e):
            i, buf, free = land.take()
            sp.wait(free)
            fetched[e] = (i, buf, land.filled(i, nc.sync.dma_start(buf[:, :, :, :], A["wffn"][e])))

        def expert_pieces(e):
            i, buf, t_in = fetched[e]
            j, dst, free = wf_ring.take()
            for a in range(3):
                for c in range(2):
                    t = split(dst[0][:, a, c, :], dst[1][:, a, c, :], buf[:, a, c, :], [t_in], free)
                    ready[e] = (j, dst, t)
                    yield
            land.release(i, t)
            if 0 < e <= E0 - 2:
                fetch(e + 2)

        def first_pieces(free):
            for q in (sp, act, dve):
                q.wait(free)
            t_gate = loaded("gate", gate_raw[:, :, :], A["gate0"])
            t_gb = loaded("gbias", gbias[:, :], A["gbias0"].broadcast_to([P, E0]))
            fetch(0)
            yield
            for _ in expert_pieces(0):
                yield
            said["gate"] = split(gate[0][:, :, :], gate[1][:, :, :], gate_raw[:, :, :], [t_gate])
            said["gbias"] = t_gb
            yield

        def gate_pieces(h, ring):
            j, ps, free = ring.take()
            pe.wait(free, said["gate"], said["t"])
            t = mm_group(ps[0:E0, :], [q for k in range(KT) for q in three(
                (gate[0][:, k, :], gate[1][:, k, :]), (xnT[h][0][:, k, :], xnT[h][1][:, k, :]))])
            act.wait(t, said.get("scT"))
            t = act.did(nc.scalar.activation(scT[:, :], ps[0:E0, :], ACT.Sigmoid))
            ring.release(j, t)
            yield
            j, ps, free = ring.take()
            pe.wait(free, t)
            for b in range(HB):
                ins = nc.tensor.transpose(ps[:, b * E0:(b + 1) * E0],
                                          scT[:, b * P:(b + 1) * P], ident[0:E0, 0:E0])
            t = said["scT"] = pe.did(ins)
            dve.wait(t, said["gbias"])
            said["scores"] = dve.did(nc.vector.tensor_tensor(
                sc[:, h * HB:(h + 1) * HB, :], ps[:, 0:HB * E0].rearrange("p (b e) -> p b e", b=HB),
                gbias[:, :].unsqueeze(1).broadcast_to([P, HB, E0]), ALU.add))
            ring.release(j, said["scores"])
            yield

        pr_ring, pT_ring, kd_ring, vp_ring = Ring(range(PR)), Ring(pT), Ring(kd), Ring(vp)
        free_of = {}
        t_q = {}

        def xn_free():
            return free_of["xn"]


        def key_pieces(ring):
            j, ps, free = ring.take()
            pe.wait(free, said["ctx"], t_w["k"])
            t = mm_group(ps[:, :], [q for k in range(KT) for q in three(
                (wkv[0][:, 0, k, :], wkv[1][:, 0, k, :]), (ctxT[0][:, k, :], ctxT[1][:, k, :]))])
            act.wait(t, t_bk, free_of.get("kT"))
            t = act.did(nc.scalar.activation(kT[0][:, :], ps[:, :], ACT.Identity, bias=bk[:, 0:1]))
            dve.wait(t)
            said["k"] = dve.did(nc.vector.scalar_tensor_tensor(
                out=kT[1][:, :], in0=ps[:, :], scalar=bk[:, 0:1], in1=kT[0][:, :].bitcast(F32),
                op0=ALU.add, op1=ALU.subtract))
            ring.release(j, said["k"])
            yield

        def value_pieces(ring):
            for b in range(HB):
                j, ps, free = ring.take()
                pe.wait(free, said["ctx"], t_w["v"])
                t = mm_group(ps[:, 0:P], [q for k in range(KT) for q in three(
                    (ctxT[0][:, k, b * P:(b + 1) * P], ctxT[1][:, k, b * P:(b + 1) * P]),
                    (wkv[0][:, 1, k, :], wkv[1][:, 1, k, :]))])
                free_of["ctx"] = t
                dve.wait(t, t_bv, free_of.get("v"))
                said["v"] = dve.did(nc.vector.tensor_tensor(v[:, b, :], ps[:, 0:P], bv[:, :], ALU.add))
                ring.release(j, said["v"])
                yield

        def query_pieces(half, ms, ring):
            dst = qT[half]
            for m in ms:
                j, ps, free = ring.take()
                pe.wait(free, said["t"], t_w["q"])
                t = mm_group(ps[:, :], [q for k in range(KT) for q in three(
                    (wq[0][:, k, m * P:(m + 1) * P], wq[1][:, k, m * P:(m + 1) * P]),
                    (xnA[0][:, k, :], xnA[1][:, k, :]))])
                free_of["xn"] = t
                act.wait(t, t_bq)
                t = act.did(nc.scalar.activation(dst[0][:, m, :], ps[:, :], ACT.Identity, bias=bq[:, m:m + 1]))
                dve.wait(t)
                t_q[half] = dve.did(nc.vector.scalar_tensor_tensor(
                    out=dst[1][:, m, :], in0=ps[:, :], scalar=bq[:, m:m + 1],
                    in1=dst[0][:, m, :].bitcast(F32), op0=ALU.add, op1=ALU.subtract))
                ring.release(j, t_q[half])
                yield

        units = [(b, kv) for b in range(B) for kv in range(KV0)]
        row, state = {}, {}

        def keys_repeat(b):
            st = row.setdefault(b, {})
            j, ps, free = y_ring.take()
            pe.wait(free, said["k"], t_sel)
            cols = slice((b % HB) * P, (b % HB + 1) * P)
            for m in range(KT):
                t = mm_group(ps[:, m * P:(m + 1) * P], [(sel[:, m, :], kT[0][:, cols]),
                                                        (sel[:, m, :], kT[1][:, cols])])
            free_of["kT"] = t
            st["kd"] = kd_ring.take()
            ps3 = ps[:, :].rearrange("p (m c) -> p m c", m=KT)
            st["rep"] = split(krep[0][:, :, :], krep[1][:, :, :], ps3, [t], free_of.get("krep"))
            y_ring.release(j, st["rep"])

        def keys_mask(b, g):
            st = row[b]
            _, buf, free = st["kd"]
            dve.wait(st["rep"], free)
            pool.wait(st["rep"], free)
            t = dve.did(nc.vector.tensor_scalar(buf[0][:, :, g, :], krep[0][:, :, :].bitcast(F32),
                                                mask[:, g:g + 1], None, ALU.mult))
            t2 = pool.did(nc.gpsimd.tensor_scalar(buf[1][:, :, g, :], krep[1][:, :, :].bitcast(F32),
                                                  mask[:, g:g + 1], 1.0, ALU.mult, ALU.mult))
            st["t_kd"] = free_of["krep"] = [t, t2]

        def values_spread(b):
            st = row[b]
            w, buf, free = st["vp"] = vp_ring.take()
            dst = [bass.AP(tensor=q.tensor, offset=q.offset, ap=[list(q.ap[0]), [P + HD0, KV0], [1, HD0]])
                   for q in (h[:, :, :].rearrange("p a c -> p (a c)") for h in buf)]
            act.wait(*t_zero)
            st["t_v"] = split(dst[0], dst[1], v[:, b % HB, :].rearrange("p (a d) -> p a d", a=KV0),
                               [said["v"]], free)
            free_of["v"] = st["t_v"]

        def scores(i):
            b, kv = units[i]
            rows, m = slice(64 * (kv % 2), 64 * (kv % 2) + 64), kv // 2
            kb = row[b]["kd"][1]
            sj, ps, free = s_ring.take()
            pe.wait(free, t_q[b // HB], row[b]["t_kd"])
            t = mm_group(ps[:, :], three(
                tuple(q[rows, m, (b % HB) * P:(b % HB + 1) * P] for q in qT[b // HB]),
                tuple(k[rows, m, :, :] for k in kb)))
            if kv == KV0 - 1:
                kd_ring.release(row[b]["kd"][0], t)
            state[i] = {"s": (sj, ps, t)}

        def softmax_max(i):
            st = state[i]
            sj, ps, t = st["s"]
            k = i % SX
            dve.wait(t)
            t = dve.did(nc.vector.tensor_reduce(sx[:, k, 0, :], ps[:, :].rearrange("p (h k) -> p h k", h=G0),
                                                AX.X, ALU.max))
            dve.wait(t)
            st["nb"] = dve.did(nc.vector.tensor_scalar(sx[:, k, 1, :], sx[:, k, 0, :], -SCALE0, None, ALU.mult))

        def softmax_exp(i):
            st = state[i]
            sj, ps, _ = st["s"]
            j, _, free = st["pr"] = pr_ring.take()
            k = i % SX
            act.wait(st["nb"], free)
            for g in range(G0):
                t = act.did(nc.scalar.activation(
                    pr[:, j, g, :], ps[:, g * P:(g + 1) * P], ACT.Exp,
                    bias=sx[:, k, 1, g:g + 1], scale=SCALE0, accum_out=sx[:, k, 2, g:g + 1]))
            s_ring.release(sj, t)
            st["e"] = t

        def softmax_norm(i):
            st = state[i]
            j, k = st["pr"][0], i % SX
            dve.wait(st["e"])
            t = dve.did(nc.vector.reciprocal(sx[:, k, 3, :], sx[:, k, 2, :]))
            pool.wait(t, st["e"])
            for g in range(G0):
                t = pool.did(nc.gpsimd.tensor_scalar(pr[:, j, g, :], pr[:, j, g, :], sx[:, k, 3, g:g + 1],
                                                     1.0, ALU.mult, ALU.mult))
            st["p"] = t

        def turn(i):
            st = state[i]
            j = st["pr"][0]
            tj, ps, free = t_ring.take()
            pe.wait(free, st["p"], t_const)
            for g in range(G0):
                ins = nc.tensor.transpose(ps[:, g * P:(g + 1) * P], pr[:, j, g, :], ident)
            t = pe.did(ins)
            pr_ring.release(j, t)
            pj, buf, free = pT_ring.take()
            t = split(buf[0][:, :], buf[1][:, :], ps[:, :], [t], free)
            t_ring.release(tj, t)
            st["pT"] = (pj, buf, t)

        def attend(i):
            b, kv = units[i]
            st = state.pop(i)
            pj, buf, t = st["pT"]
            if kv == 0:
                row[b]["o"] = o_ring.take()
            oj, ops, free = row[b]["o"]
            w, vbuf, _ = row[b]["vp"]
            pe.wait(t, row[b]["t_v"], free)
            for n, (a_, c_) in enumerate(three((vbuf[0][:, kv, :], vbuf[1][:, kv, :]),
                                               (buf[0][:, :], buf[1][:, :]))):
                ins = nc.tensor.matmul(ops[:, :], a_, c_, start=(kv == 0 and n == 0),
                                       stop=(kv == KV0 - 1 and n == 2))
            t = pe.did(ins)
            pT_ring.release(pj, t)
            if kv == KV0 - 1:
                vp_ring.release(w, t)
                row[b]["a"] = split(aT[0][:, :], aT[1][:, :], ops[:, :], [t], free_of.get("aT"))
                o_ring.release(oj, row[b]["a"])

        def project_out(b):
            yj, yps, yfree = y_ring.take()
            pe.wait(yfree, row[b]["a"], t_w["o"])
            t = mm_group(yps[:, :], [q for g in range(G0) for q in three(
                (aT[0][:, g * P:(g + 1) * P], aT[1][:, g * P:(g + 1) * P]),
                (wo[0][:, g, :], wo[1][:, g, :]))])
            free_of["aT"] = t
            dve.wait(t, x_ready[b])
            t = dve.did(nc.vector.tensor_tensor(x[:, b, :], yps[:, :], x[:, b, :], ALU.add))
            x_ready[b] = t
            y_ring.release(yj, t)

        run(context_pieces(t_ctx, None))
        t_w["v"] = split(wkv[0][:, 1], wkv[1][:, 1], small_raw[:, 1], [t_kv[1]])
        norm = norm_pieces(range(HB), xnA, banks, None, said)

        def query_weight(k):
            t_w["q"] = split(wq[0][:, k, :], wq[1][:, k, :], w_raw[:, k, :], [t_wq], lo_on=pool)

        run(key_pieces(banks))
        run(norm, 1)
        keys_repeat(0)
        values = value_pieces(banks)
        for k in range(KT):
            run(values, 1)
            run(norm, 1)
            keys_mask(0, k)
            if k < 2:
                query_weight(2 * k)
                query_weight(2 * k + 1)
        run(norm)
        values_spread(0)
        run(query_pieces(0, range(KT), banks))
        run(bias_pieces(0))
        pr_ring.release(0, t_w["k"])
        pr_ring.release(1, t_w["v"])
        pr_ring.release(2, t_sel)
        sp.wait(said["ctx"])
        nc.sync.dma_start(ctxT_raw[:, :, :], A["ctxT"][1]).then_inc(s_ctx[0], 16)
        t_ctx = [(s_ctx[0], 32)] * 2
        sp.wait(t_w["q"])
        t_wo = loaded("wo0", w_raw[:, :, :], A["wo0"])

        def output_weight_pieces():
            for k in range(KT):
                t_w["o"] = split(wo[0][:, k, :], wo[1][:, k, :], w_raw[:, k, :], [t_wo])
                yield

        for n in range(4):
            ring, k = (s_ring, n) if n < 3 else (t_ring, 0)
            ring.release(k, banks.reader[n])

        LEAD, LAG_T, LAG_A = 2, 2, 3
        second = chain(output_weight_pieces(), context_pieces(t_ctx, free_of["ctx"]),
                       norm_pieces(range(HB, B), xnA, t_ring, xn_free, said), bias_pieces(1),
                       query_pieces(1, [0], t_ring))
        second_keys = chain(key_pieces(t_ring), value_pieces(t_ring), query_pieces(1, range(1, KT), t_ring))
        n_units = len(units)
        half_units = n_units // 2
        for i in range(-LEAD, n_units + LAG_A + 1):
            b, kv = divmod(i, KV0)
            if i + LEAD < n_units:
                scores(i + LEAD)
            if 1 <= i <= n_units:
                softmax_norm(i - 1)
            if i + LEAD < n_units:
                softmax_max(i + LEAD)
            if 0 <= i < n_units:
                softmax_exp(i)
            if LAG_T <= i < n_units + LAG_T:
                turn(i - LAG_T)
            if LAG_A <= i < n_units + LAG_A:
                attend(i - LAG_A)
            if 0 <= b < B - 1:
                if kv == 0:
                    keys_repeat(b + 1)
                if kv == LAG_A:
                    values_spread(b + 1)
                if 1 <= kv < 1 + G0:
                    keys_mask(b + 1, kv - 1)
            if i < 1:
                pass
            elif i < half_units - KV0 - LAG_A - 1:
                run(second, 1)
            elif i < half_units - LEAD - 1:
                run(second)
                run(second_keys, 1)
            elif i == half_units - LEAD - 1:
                run(second_keys)
            elif i == half_units + LAG_A:
                ahead = chain(first_pieces(now()), norm_pieces(range(HB), xnA, t_ring, xn_free, said),
                              gate_pieces(0, t_ring))
            elif i % 2 == 0 and i > half_units + LAG_A:
                run(ahead, 1)
            if i > LAG_A and (i - LAG_A) % KV0 == 0:
                project_out((i - LAG_A) // KV0 - 1)
        s_reader, t_reader, o_reader, y_reader = (r.reader for r in (s_ring, t_ring, o_ring, y_ring))

        run(ahead)
        attended = now()
        for q in (act, dve, pool, sp):
            q.wait(attended)
        for n, token in enumerate([*s_reader, *t_reader, *o_reader, *y_reader]):
            (up if n < 4 else down).release(n % 4, token)
        fetch(1)
        fetch(2)

        def hidden(e, h):
            j, w, t_w_ = ready[e]
            zj, zbuf, zfree = zs_ring.take()
            for it in range(IT):
                pss = []
                for a in range(2):
                    uj, ps, free = up.take()
                    pe.wait(free, t_w_, t_xn[h])
                    def wcol(part, k):
                        return w[part][:, a, k // 2, (k % 2) * I0 + it * P:(k % 2) * I0 + (it + 1) * P]
                    t = mm_group(ps[:, :], [q for k in range(KT) for q in three(
                        (wcol(0, k), wcol(1, k)), (xnT[h][0][:, k, :], xnT[h][1][:, k, :]))])
                    pss.append((uj, ps, t))
                (gj, gps, gt), (uj, ups, ut) = pss
                sj, sbuf, sfree = silu_ring.take()
                act.wait(gt, sfree)
                t_s = act.did(nc.scalar.activation(sbuf[:, :], gps[:, :], ACT.Silu))
                up.release(gj, t_s)
                qj, qbuf, qfree = z_ring.take()
                dve.wait(t_s, ut, qfree)
                t_z = dve.did(nc.vector.tensor_tensor(qbuf[:, :], ups[:, :], sbuf[:, :], ALU.mult))
                up.release(uj, t_z)
                silu_ring.release(sj, t_z)
                t = split(zbuf[0][:, it, :], zbuf[1][:, it, :], qbuf[:, :], [t_z], zfree)
                z_ring.release(qj, t)
            return zj, zbuf, t

        def output(e, h, zj, zbuf, t_z):
            j, w, t_w_ = ready[e]
            for b in range(HB):
                dj, ps, free = down.take()
                pe.wait(free, t_z, t_w_)
                t = mm_group(ps[:, :], [q for it in range(IT) for q in three(
                    (zbuf[0][:, it, b * P:(b + 1) * P], zbuf[1][:, it, b * P:(b + 1) * P]),
                    (w[0][:, 2, it, :], w[1][:, 2, it, :]))])
                tile = h * HB + b
                dve.wait(t, x_ready[tile])
                if e == 0:
                    t = dve.did(nc.vector.tensor_tensor(x[:, tile, :], ps[:, :], x[:, tile, :], ALU.add))
                else:
                    dve.wait(t_cw)
                    t = dve.did(nc.vector.scalar_tensor_tensor(
                        out=x[:, tile, :], in0=ps[:, :], scalar=cw[:, tile, e - 1:e],
                        in1=x[:, tile, :], op0=ALU.mult, op1=ALU.add))
                x_ready[tile] = t
                down.release(dj, t)
                yield
            zs_ring.release(zj, pe.last())
            if h == 1:
                wf_ring.release(j, pe.last())

        def top(src, mx_, idx, idxf, onehot, k, n_exp, t, n):
            dve.wait(t)
            for b in range(n):
                t = dve.did(nc.vector.max(mx_[:, b, :], src[:, b, :]))
            dve.wait(t)
            for b in range(n):
                t = dve.did(nc.vector.max_index(idx[:, b, :], mx_[:, b, :], src[:, b, :]))
            dve.wait(t)
            t = dve.did(nc.vector.tensor_copy(idxf[:, :, :], idx[:, :, 0:k]))
            dve.wait(t, t_const)
            return dve.did(nc.vector.tensor_tensor(
                onehot[:, :, :, :], idxf[:, :, :].unsqueeze(3).broadcast_to([P, n, k, n_exp]),
                iota[:, 0:n_exp].unsqueeze(1).unsqueeze(1).broadcast_to([P, n, k, n_exp]), ALU.is_equal))

        def routing():
            t = top(sc, mx, mi_, mif, oh, TOP0, E0, said["scores"], B)
            dve.wait(t)
            t = dve.did(nc.vector.tensor_reduce(cw[:, :, :], oh[:, :, :, :].rearrange("p b k e -> p b e k"),
                                                AX.X, ALU.add))
            dve.wait(t)
            t = dve.did(nc.vector.tensor_tensor(cw[:, :, :], cw[:, :, :], sc[:, :, :], ALU.mult))
            t2 = dve.did(nc.vector.tensor_reduce(ssum[:, :], mx[:, :, 0:TOP0], AX.X, ALU.add))
            dve.wait(t2)
            t2 = dve.did(nc.vector.tensor_scalar(ssum[:, :], ssum[:, :], 1e-20, None, ALU.add))
            dve.wait(t2)
            t2 = dve.did(nc.vector.reciprocal(ssum[:, :], ssum[:, :]))
            dve.wait(t2)
            t_cw = dve.did(nc.vector.tensor_tensor(
                cw[:, :, :], cw[:, :, :], ssum[:, :].unsqueeze(2).broadcast_to([P, B, E0]), ALU.mult))
            return t_cw

        place[0] = PHASE
        v = pair("v1", [P, 2, HB, D])
        outw = [pair(f"w1o{i}", [P, D]) for i in range(UH, 2 * UH)]
        qT = [None, pair("q1T1", [P, UH, HT])]
        aT = pair("a1T", [P, UH * P])
        pT = pair("p1T", [P, 2, UH * P])
        pr = [sb(f"p1_{i}", [P, UH, 2 * P]) for i in range(2)]
        k1_at, K1_BYTES = place[0], 2 * HT * 4
        kT = pair("k1T", [P, KV1, 2, HT])
        place[0] = w1_at = max(place[0], above_experts)
        head = [pair(f"w1q{i}", [P, KT, P]) for i in range(4)]
        raw1 = [sb(f"w1_raw{i}", [P, D]) for i in range(3)]
        qT[0] = pair("q1T0", [P, UH, HT])
        w1_end = place[0]
        outw = [pair(f"w1o{i}", [P, D]) for i in range(UH)] + outw
        mx1 = [sb(f"mx1_{i}", [P, 4 * UH]) for i in range(4)]

        land1 = Landing(raw1, [sem(f"ld_w1{i}") for i in range(3)])
        head_ring, out_ring = Ring(head), Ring(outw)
        s_ring = Ring(bank[0:4])
        to_ring, y_ring = Ring(bank[4:6]), Ring(bank[6:8])
        pr_ring = Ring(pr)
        q_free = [None, None]
        kT_free = [None] * KV1
        v_free = [None] * HB
        pT_free = [None, None]
        free_of = {}

        def step_weights(u, b):
            n = UH * u + b + UH + 2
            w = [("wq1", n, head_ring)] if n < H1 else []
            if b >= 2 and u + 1 < UNITS:
                w += [("wo1", UH * (u + 1) + 2 * (b - 2) + h, out_ring) for h in range(2)]
            return w

        stream = []
        for half in range(2):
            stream += [("wk1", g, head_ring) for g in range(KV1)]
            stream += [("ctxT", (half, k), None) for k in range(KT)]
            stream += [("wv1", k, out_ring) for k in range(KT)]
            stream += [("wq1", h, head_ring) for h in range(UH)]
            for h in range(UH):
                stream += [("wq1", UH + h, head_ring)] if h < 2 else []
                stream += [("wo1", h, out_ring)]
            for u in range(UNITS):
                for b in range(HB):
                    stream += step_weights(u, b)
        loads, splits = list(stream), []
        have = {"head": [], "out": []}

        def fetch_weight():
            if loads:
                name, n, ring = loads.pop(0)
                i, buf, free = land1.take()
                sp.wait(free)
                src = A[name][n[0]][:, n[1], :] if name == "ctxT" else A[name][n]
                t = land1.filled(i, nc.sync.dma_start(buf[:, :], src))
                splits.append((name, n, ring, i, buf, t))

        def weight():
            if not splits:
                return
            name, n, ring, i, buf, t_in = splits.pop(0)
            if name == "ctxT":
                k = n[1]
                hi, lo, free = qT[0][0][:, k, :], qT[0][1][:, k, :], q_free[0]
            else:
                j, dst, free = ring.take()
                hi, lo = (q[:, :, :].rearrange("p k c -> p (k c)") if ring is head_ring else q[:, :] for q in dst)
            t = split(hi, lo, buf[:, :], [t_in], free)
            land1.release(i, t)
            if name == "ctxT":
                said["ctx1"] = t
            else:
                have["head" if ring is head_ring else "out"].append((j, dst, t))
            fetch_weight()

        def project(w, t_w_, src, t_src, dst, dst_free, ring):
            sj, ps, free = ring.take()
            pe.wait(free, t_w_, *t_src)
            t = mm_group(ps[:, :], [q for k in range(KT) for q in three(
                (w[0][:, k, :], w[1][:, k, :]), (src[0][:, k, :], src[1][:, k, :]))])
            t2 = split(dst[0], dst[1], ps[:, :], [t], dst_free)
            ring.release(sj, t2)
            return t, t2

        def opening_pieces(half, norm, ring):
            ctxT = qT[0]
            for k in range(2 * KT):
                weight()
                if k % 2 == 1:
                    yield
            wk = have["head"]
            have["head"] = []
            t_c = said["ctx1"]

            def keys(g, part, src, t_src):
                t, t2 = project(wk[g][1], wk[g][2], src, [t_src],
                                (kT[0][:, g, part, :], kT[1][:, g, part, :]), kT_free[g], ring)
                said["keys"] = t2
                if part == 1:
                    head_ring.release(wk[g][0], t)

            for g in range(KV1 - 1):
                keys(g, 0, ctxT, t_c)
                run(norm, 1)
                yield
            for _ in norm:
                yield
            for g in range(KV1 - 1):
                keys(g, 1, xnA, said["t"])
                weight()
                yield
            keys(KV1 - 1, 0, ctxT, t_c)
            weight()
            yield
            keys(KV1 - 1, 1, xnA, said["t"])
            yield

        def value_tile(part, b, ring):
            wv = said["wv"]
            src, t_src = (qT[0], said["ctx1"]) if part == 0 else (xnA, said["t"])
            cols = slice(b * P, (b + 1) * P)
            sj, ps, free = ring.take()
            pe.wait(free, t_src, *[w[2] for w in wv])
            t = mm_group(ps[:, :], [q for k in range(KT) for q in three(
                (src[0][:, k, cols], src[1][:, k, cols]), (wv[k][1][0][:, :], wv[k][1][1][:, :]))])
            t_v[b] = split(v[0][:, part, b, :], v[1][:, part, b, :], ps[:, :], [t], v_free[b])
            ring.release(sj, t_v[b])
            return t

        def value_pieces(ring):
            said["wv"] = have["out"][-KT:]
            del have["out"][-KT:]
            for b in range(HB):
                weight()
                q_free[0] = value_tile(0, b, ring)
                yield

        def latent_pieces(ring):
            for b in range(HB):
                t = value_tile(1, b, ring)
                if b == HB - 1:
                    for w in said["wv"]:
                        out_ring.release(w[0], t)
                yield

        state, t_qs, t_v = {}, {}, {}

        def query(half, n):
            u, h = divmod(n, UH)
            j, w, t_w_ = have["head"].pop(0)
            dst = qT[u % 2]
            t, t2 = project(w, t_w_, xnA, [said["t"]], (dst[0][:, h, :], dst[1][:, h, :]), q_free[u % 2],
                            y_ring)
            head_ring.release(j, t)
            free_of["xn"] = t
            if h == UH - 1:
                t_qs[u] = t2

        steps = [(u, b) for u in range(UNITS) for b in range(HB)]

        def scores(i):
            u, b = steps[i]
            g = u * UH // (H1 // KV1)
            tok = slice(b * P, (b + 1) * P)
            q = qT[u % 2]
            st = state[i] = {"s": []}
            for pr_ in range(UH // 2):
                sj, ps, free = s_ring.take()
                pe.wait(free, t_qs[u], t_keys)
                for hh in range(2):
                    h = 2 * pr_ + hh
                    t = mm_group(ps[:, hh * 2 * P:(hh + 1) * 2 * P], three(
                        (q[0][:, h, tok], q[1][:, h, tok]),
                        (kT[0][:, g, :, tok], kT[1][:, g, :, tok])))
                st["s"].append((sj, ps, t))
            kT_free[g] = t
            if b == HB - 1:
                q_free[u % 2] = t

        def softmax_max(i):
            st = state[i]
            m = mx1[i % 4]
            for n, (_, ps, t) in enumerate(st["s"]):
                dve.wait(t)
                t = dve.did(nc.vector.tensor_reduce(
                    m[:, 2 * n:2 * n + 2], ps[:, :].rearrange("p (h k) -> p h k", h=2), AX.X, ALU.max))
            dve.wait(t)
            st["nb"] = dve.did(nc.vector.tensor_scalar(m[:, UH:2 * UH], m[:, 0:UH], -SCALE1, None, ALU.mult))

        def softmax_exp(i):
            st = state[i]
            st["j"], _, free = pr_ring.take()
            j, m = st["j"], mx1[i % 4]
            act.wait(st["nb"], free)
            for n, (sj, ps, _) in enumerate(st["s"]):
                for hh in range(2):
                    h = 2 * n + hh
                    t = act.did(nc.scalar.activation(
                        pr[j][:, h, :], ps[:, hh * 2 * P:(hh + 1) * 2 * P], ACT.Exp,
                        bias=m[:, UH + h:UH + h + 1], scale=SCALE1,
                        accum_out=m[:, 2 * UH + h:2 * UH + h + 1]))
                s_ring.release(sj, t)
            st["e"] = t

        def softmax_norm(i):
            st = state[i]
            j, m = st["j"], mx1[i % 4]
            dve.wait(st["e"])
            t = dve.did(nc.vector.reciprocal(m[:, 3 * UH:4 * UH], m[:, 2 * UH:3 * UH]))
            pool.wait(t, st["e"])
            for h in range(UH):
                t = pool.did(nc.gpsimd.tensor_scalar(
                    pr[j][:, h, :], pr[j][:, h, :], m[:, 3 * UH + h:3 * UH + h + 1],
                    1.0, ALU.mult, ALU.mult))
            st["p"] = t

        def turn(i, part):
            st = state[i]
            tj, ps, free = to_ring.take()
            pe.wait(free, st["p"], t_const)
            for h in range(UH):
                ins = nc.tensor.transpose(ps[:, h * P:(h + 1) * P],
                                          pr[st["j"]][:, h, part * P:(part + 1) * P], ident)
            t = pe.did(ins)
            t2 = split(pT[0][:, part, :], pT[1][:, part, :], ps[:, :], [t], pT_free[part])
            to_ring.release(tj, t2)
            st.setdefault("pT", []).append(t2)
            if part == 1:
                pr_ring.release(st["j"], t)

        def attend(i):
            st = state[i]
            u, b = steps[i]
            g = u * UH // (H1 // KV1)
            oj, ps, free = to_ring.take()
            pe.wait(free, t_v[b])
            prs = []
            for part in range(2):
                vv = tuple(q[:, part, b, g * P:(g + 1) * P] for q in v)
                prs += three(vv, (pT[0][:, part, :], pT[1][:, part, :]))
            for n, (a, c) in enumerate(prs):
                pe.wait(st["pT"][n // 3])
                ins = nc.tensor.matmul(ps[:, :], a, c, start=(n == 0), stop=(n == 5))
                if n % 3 == 2:
                    t = pT_free[n // 3] = pe.did(ins)
            t2 = split(aT[0][:, :], aT[1][:, :], ps[:, :], [t], free_of.get("aT"))
            to_ring.release(oj, t2)
            v_free[b] = t
            st["a"] = t2

        def project_out(half, i):
            st = state.pop(i)
            u, b = steps[i]
            if b == 0:
                wos[u] = [have["out"].pop(0) for _ in range(UH)]
            ws = wos[u]
            yj, ps, free = y_ring.take()
            pe.wait(free, st["a"], *[w[2] for w in ws])
            t = mm_group(ps[:, :], [q for h in range(UH) for q in three(
                (aT[0][:, h * P:(h + 1) * P], aT[1][:, h * P:(h + 1) * P]),
                (ws[h][1][0][:, :], ws[h][1][1][:, :]))])
            free_of["aT"] = t
            if b == HB - 1:
                for w in ws:
                    out_ring.release(w[0], t)
            tile = half * HB + b
            dve.wait(t, x_ready[tile])
            t = dve.did(nc.vector.tensor_tensor(x[:, tile, :], ps[:, :], x[:, tile, :], ALU.add))
            x_ready[tile] = t
            y_ring.release(yj, t)

        t_xn = [said["t"], None]
        norm = norm_pieces(range(HB, B), xnB, down, None, said)
        run(norm, 3)
        before = None
        for e in range(E0):
            for h in range(2):
                z_ = hidden(e, h)
                before = before and run(output(*before))
                if (e, h) == (0, 0):
                    products = output(0, 0, *z_)
                    for _ in range(HB):
                        run(norm, 1)
                        run(products, 1)
                    run(norm)
                    run(products)
                    t_xn[1] = said["t"]
                    gate_half = gate_pieces(1, down)
                    run(gate_half, 1)
                if (e, h) == (0, 1):
                    run(gate_half)
                    t_cw = routing()
                before = (e, h, *z_) if (e, h) != (0, 0) else None
                if h == 0 and e + 1 <= E0:
                    run(expert_pieces(e + 1))

        routed = now()
        for ring in (head_ring, out_ring):
            for n in range(4):
                ring.release(n, routed)
        q_free[0] = routed
        for _ in raw1:
            fetch_weight()
        opening = opening_pieces(0, norm_pieces(range(HB), xnA, s_ring, xn_free, said), s_ring)
        z_ = hidden(E0, 0)
        run(output(*before))
        kT_free[:] = [now()] * KV1
        run(opening, 4)
        before = (E0, 0, *z_)
        z_ = hidden(E0, 1)
        for n in range(4):
            s_ring.release(n, up.reader[n])
        free_of["xn"] = now()
        run(output(*before))
        v_free[:] = [now()] * HB
        products = output(E0, 1, *z_)
        run(opening, 3)
        for _ in range(HB):
            run(opening, 2)
            run(products, 1)
        run(products)
        for n in range(4):
            (to_ring if n < 2 else y_ring).release(n % 2, down.reader[n])
        ffn_done = now()
        for n in range(UH, 2 * UH):
            out_ring.release(n, ffn_done)
        for n in range(2):
            pr_ring.release(n, ffn_done)
        q_free[1] = free_of["aT"] = ffn_done
        pT_free[:] = [ffn_done] * 2

        place[0] = w1_at
        wm, wm_raw = pair("wm", [P, KT, D]), sb("wm_raw", [P, KT, D])
        ws, ws_raw = pair("ws", [P, KT, SMALL]), sb("ws_raw", [P, KT, SMALL])
        lb, lb_raw = pair("lb", [P, D]), sb("lb_raw", [P, D])
        assert place[0] <= w1_end
        place[0] = k1_at
        vecs = sb("vecs", [P, 2 * G1 + E1])
        gw2 = sb("gw2", [P, E1, G1])
        gb1 = sb("gb1", [G1, 1])
        ones = sb("ones", [P, P])[:, :]
        hT = [sb(f"hT{h}", [G1, HT]) for h in range(2)]
        h_ = sb("h_", [P, B, G1])
        hst = sb("hst", [P, B, 6])
        hmv = sb("hmv", [P, B, 2])
        hr = sb("hr", [P, B])
        gates = sb("gates", [P, B, E1])
        gmx = sb("gmx", [P, B, 8])
        gmi = sb("gmi", [P, B, 8], U32)
        gmif = sb("gmif", [P, B, TOP1])
        goh = sb("goh", [P, B, TOP1, E1])
        assert place[0] <= k1_at + 3 * K1_BYTES
        place[0] = k1_at + 4 * K1_BYTES
        gk = sb("gk", [P, B, TOP1])
        gks = sb("gks", [P, B])
        gw = sb("gw", [P, B, TOP1, E1])
        chosen = sb("chosen", [P, TOP1, E1])
        allowed = sb("allowed", [P, TOP1, E1])
        prod = sb("prod", [P, HB, E1, G1])
        tmpT = [sb(f"tmpT{h}", [P, HT]) for h in range(2)]
        assert place[0] <= k1_at + 7 * K1_BYTES
        place[0] = PHASE
        xnB1 = pair("xnB1", [P, KT, HT])
        we = [sb(f"we{h}", [P, HB, E1, R1]) for h in range(2)]
        tw = [sb(f"tw{h}", [P, HT]) for h in range(2)]
        la = [pair(f"la{h}", [P, HT]) for h in range(2)]
        assert place[0] <= k1_at
        xn1 = [xnA, xnB1]
        t_xn1 = [None, None]
        TT, TS = nc.vector.tensor_tensor, nc.vector.tensor_scalar

        def weight_pieces(free):
            for q in (sp, act, dve, pool):
                q.wait(free)
            t_s = loaded("ws", ws_raw[:, :, :], A["ws1"])
            t_gb1 = loaded("gb1", gb1[:, :], A["gb1"])
            t_m = loaded("wm", wm_raw[:, :, :], A["wm1"])
            said["vecs"] = loaded("vecs", vecs[:, :], A["vecs1"].broadcast_to([P, 2 * G1 + E1]))
            said["gw2"] = loaded("gw2", gw2[:, :, :], A["gw2"].broadcast_to([P, E1, G1]))
            t_l = loaded("lb", lb_raw[:, :], A["lb1"])
            said["gb1"] = t_gb1
            said["ones"] = pool.did(nc.gpsimd.memset(ones, 1.0))
            yield
            said["ws"] = split(ws[0][:, :, :], ws[1][:, :, :], ws_raw[:, :, :], [t_s])
            yield
            for k in range(KT):
                said["wm"] = split(wm[0][:, k, :], wm[1][:, k, :], wm_raw[:, k, :], [t_m])
                yield
            said["lb"] = split(lb[0][:, :], lb[1][:, :], lb_raw[:, :], [t_l])
            yield

        def small_pieces(h, ring):
            j, ps, free = ring.take()
            pe.wait(free, t_xn1[h], said["ws"])
            t = mm_group(ps[0:G1, :], [q for k in range(KT) for q in three(
                (ws[0][:, k, P:SMALL], ws[1][:, k, P:SMALL]), (xn1[h][0][:, k, :], xn1[h][1][:, k, :]))])
            act.wait(t, said["gb1"])
            t = act.did(nc.scalar.activation(hT[h][:, :], ps[0:G1, :], ACT.Identity, bias=gb1[:, 0:1]))
            ring.release(j, t)
            yield
            j, ps, free = ring.take()
            pe.wait(free)
            t_a = mm_group(ps[:, :], [q for k in range(KT) for q in three(
                (ws[0][:, k, 0:P], ws[1][:, k, 0:P]), (xn1[h][0][:, k, :], xn1[h][1][:, k, :]))])
            act.wait(t_a)
            said["tmpT", h] = act.did(nc.scalar.activation(tmpT[h][:, :], ps[:, :], ACT.Copy))
            ring.release(j, said["tmpT", h])
            j, ps, free = ring.take()
            pe.wait(free, t)
            for b in range(HB):
                ins = nc.tensor.transpose(ps[:, b * G1:(b + 1) * G1], hT[h][:, b * P:(b + 1) * P],
                                          ident[0:G1, 0:G1])
            t = pe.did(ins)
            dve.wait(t)
            said["h"] = dve.did(nc.vector.tensor_copy(
                h_[:, h * HB:(h + 1) * HB, :], ps[:, 0:HB * G1].rearrange("p (b c) -> p b c", b=HB)))
            ring.release(j, said["h"])
            yield

        def gating_pieces(h):
            bs = slice(h * HB, (h + 1) * HB)
            tiles = range(h * HB, (h + 1) * HB)

            def step(ins):
                t = dve.did(ins)
                dve.wait(t)
                return t

            def row(k0, n):
                return vecs[:, k0:k0 + n].unsqueeze(1).broadcast_to([P, HB, n])

            dve.wait(said["h"])
            for b in tiles:
                t = dve.did(nc.vector.bn_stats(hst[:, b, :], h_[:, b, :]))
            dve.wait(t)
            for b in tiles:
                t = dve.did(nc.vector.bn_aggr(hmv[:, b, :], hst[:, b, :]))
            act.wait(t)
            t = act.did(nc.scalar.activation(hr[:, bs], hmv[:, bs, 1], ACT.Sqrt, bias=eps))
            yield
            dve.wait(t)
            step(nc.vector.reciprocal(hr[:, bs], hr[:, bs]))
            for b in tiles:
                t = dve.did(TS(h_[:, b, :], h_[:, b, :], hmv[:, b, 0:1], hr[:, b:b + 1], ALU.subtract, ALU.mult))
            dve.wait(t, said["vecs"], said["gw2"])
            step(TT(h_[:, bs, :], h_[:, bs, :], row(0, G1), ALU.mult))
            step(TT(h_[:, bs, :], h_[:, bs, :], row(G1, G1), ALU.add))
            step(TS(h_[:, bs, :], h_[:, bs, :], 0.0, None, ALU.max))
            yield
            step(TT(prod[:, :, :, :], h_[:, bs, :].unsqueeze(2).broadcast_to([P, HB, E1, G1]),
                    gw2[:, :, :].unsqueeze(1).broadcast_to([P, HB, E1, G1]), ALU.mult))
            step(nc.vector.tensor_reduce(gates[:, bs, :], prod[:, :, :, :], AX.X, ALU.add))
            t = step(TT(gates[:, bs, :], gates[:, bs, :], row(2 * G1, E1), ALU.add))
            yield
            t = said["oh", h] = top(gates[:, bs, :], gmx[:, bs, :], gmi[:, bs, :], gmif[:, bs, :],
                                    goh[:, bs, :, :], TOP1, E1, t, HB)
            t = dve.did(TT(gk[:, bs, :], gmx[:, bs, 0:TOP1], gmx[:, bs, 0:1].broadcast_to([P, HB, TOP1]), ALU.subtract))
            act.wait(t)
            t = act.did(nc.scalar.activation(gk[:, bs, :], gk[:, bs, :], ACT.Exp))
            yield
            dve.wait(t)
            step(nc.vector.tensor_reduce(gks[:, bs], gk[:, bs, :], AX.X, ALU.add))
            step(nc.vector.reciprocal(gks[:, bs], gks[:, bs]))
            step(TT(gk[:, bs, :], gk[:, bs, :], gks[:, bs].unsqueeze(2).broadcast_to([P, HB, TOP1]), ALU.mult))
            said["gw", h] = step(TT(gw[:, bs, :, :], goh[:, bs, :, :],
                                    gk[:, bs, :].unsqueeze(3).broadcast_to([P, HB, TOP1, E1]), ALU.mult))
            yield

        def dense_groups(b):
            h, cols = b // HB, slice((b % HB) * P, (b % HB + 1) * P)
            return [q for k in range(KT) for q in three(
                (xn1[h][0][:, k, cols], xn1[h][1][:, k, cols]), (wm[0][:, k, :], wm[1][:, k, :]))]

        def dense(b, ring):
            j, ps, free = ring.take()
            pe.wait(free, t_xn1[0], said["wm"])
            t = mm_group(ps[:, :], dense_groups(b))
            dve.wait(t, x_ready[b])
            x_ready[b] = dve.did(TT(x[:, b, :], ps[:, :], x[:, b, :], ALU.add))
            ring.release(j, x_ready[b])

        def dense_open(b, ring):
            j, ps, free = ring.take()
            pe.wait(free, t_xn1[1], said["wm"])
            for n, (a, c) in enumerate(dense_groups(b)):
                nc.tensor.matmul(ps[:, :], a, c, start=(n == 0), stop=False)
            return j, ps

        def allowed_weights(ring):
            dve.wait(said["oh", 0], said["oh", 1])
            t = dve.did(nc.vector.tensor_reduce(chosen[:, :, :], goh[:, :, :, :].rearrange("p b k e -> p k e b"),
                                                AX.X, ALU.add))
            j, ps, free = ring.take()
            pe.wait(free, said["ones"], t)
            t = mm_group(ps[:, 0:TOP1 * E1], [(ones, chosen[:, :, :].rearrange("p k e -> p (k e)"))])
            dve.wait(t, said["gw", 0], said["gw", 1])
            t = dve.did(TS(allowed[:, :, :], ps[:, 0:TOP1 * E1].rearrange("p (k e) -> p k e", k=TOP1),
                           float(CAPACITY), 1.0 / R1, ALU.is_le, ALU.mult))
            ring.release(j, t)
            dve.wait(t)
            t = dve.did(TT(gw[:, :, :, :], gw[:, :, :, :],
                           allowed[:, :, :].unsqueeze(1).broadcast_to([P, B, TOP1, E1]), ALU.mult))
            dve.wait(t)
            for h in range(2):
                bs = slice(h * HB, (h + 1) * HB)
                said["we", h] = dve.did(TT(
                    we[h][:, :, :, :], gw[:, bs, 0, :].unsqueeze(3).broadcast_to([P, HB, E1, R1]),
                    gw[:, bs, 1, :].unsqueeze(3).broadcast_to([P, HB, E1, R1]), ALU.add))

        def weighted(h, ring):
            j, ps, free = ring.take()
            pe.wait(free, said["we", h])
            for b in range(HB):
                ins = nc.tensor.transpose(ps[:, b * P:(b + 1) * P],
                                          we[h][:, b, :, :].rearrange("p e r -> p (e r)"), ident)
            t = pe.did(ins)
            dve.wait(t, said["tmpT", h])
            t = dve.did(TT(tw[h][:, :], ps[:, :], tmpT[h][:, :], ALU.mult))
            ring.release(j, t)
            said["la", h] = split(la[h][0][:, :], la[h][1][:, :], tw[h][:, :], [t])

        s_out = sem("stored")

        def lora(b, ring, held):
            h, cols = b // HB, slice((b % HB) * P, (b % HB + 1) * P)
            if held:
                j, ps = held
            else:
                j, ps, free = ring.take()
                pe.wait(free)
            pe.wait(said["la", h], said["lb"])
            prs = three((la[h][0][:, cols], la[h][1][:, cols]), (lb[0][:, :], lb[1][:, :]))
            for n, (a, c) in enumerate(prs):
                ins = nc.tensor.matmul(ps[:, :], a, c, start=(n == 0 and not held), stop=(n == 2))
            t = pe.did(ins)
            dve.wait(t, x_ready[b])
            t = dve.did(TT(x[:, b, :], ps[:, :], x[:, b, :], ALU.add))
            if not held:
                ring.release(j, t)
            sp.wait(t)
            nc.sync.dma_start(out[b], x[:, b, :]).then_inc(s_out, 16)

        opening_at = {-5: 1, -4: 1, -3: 1, -2: 1, -1: 3, 0: 3, 1: 3}
        for half in range(2):
            run(opening)
            run(value_pieces(s_ring))
            wos = {}
            for n in range(UH):
                query(half, n)
                weight()
                if n < 2:
                    weight()
            query(half, UH)
            t_keys = said["keys"]
            latents = latent_pieces(y_ring)
            n_steps = len(steps)
            for i in range(-1, n_steps + 2):
                u, b = steps[i] if 0 <= i < n_steps else (UNITS, 0)
                if i + 1 < n_steps:
                    scores(i + 1)
                    softmax_max(i + 1)
                if 1 <= i <= n_steps:
                    turn(i - 1, 0)
                if 0 <= i < n_steps and i + UH + 1 < H1:
                    query(half, i + UH + 1)
                if 1 <= i <= n_steps:
                    turn(i - 1, 1)
                if i + 1 < n_steps:
                    softmax_exp(i + 1)
                if i >= 2:
                    project_out(half, i - 2)
                if i + 1 < n_steps:
                    softmax_norm(i + 1)
                run(latents, 1)
                if 0 <= i < n_steps:
                    for _ in step_weights(u, b):
                        weight()
                if 1 <= i <= n_steps:
                    attend(i - 1)
                if half == 0:
                    if i == n_steps - 10:
                        norm = norm_pieces(range(HB, B), xnA, y_ring, xn_free, said)
                        opening = opening_pieces(1, norm, y_ring)
                    if i in (n_steps - 10, n_steps - 8, n_steps - 6):
                        run(norm, 1)
                    run(opening, opening_at.get(i - n_steps, 0))
                else:
                    if i == n_steps - 10:
                        norm = norm_pieces(range(HB), xnA, y_ring, xn_free, said)
                    if i in (n_steps - 10, n_steps - 8, n_steps - 6):
                        run(norm, 1)
                    if i == n_steps - 5:
                        weights = weight_pieces(now())
                        run(weights, 1)
                    if n_steps - 4 <= i < n_steps:
                        run(norm, 1)
                        run(weights, 2)
                    if i == n_steps - 1:
                        run(norm)
                        run(weights)
                        t_xn1[0] = said["t"]
                        closing = small_pieces(0, y_ring)
                        norm = norm_pieces(range(HB, B), xnB1, y_ring, now, said)
                        run(norm, 1)
                    if i >= n_steps:
                        run(closing, 1)

        run(closing)
        for b in range(HB):
            run(norm, 1)
            dense(b, s_ring)
        run(norm)
        t_xn1[1] = said["t"]
        run(gating_pieces(0))
        run(small_pieces(1, y_ring))
        gating, held = gating_pieces(1), []
        for b in range(HB, B - 1):
            run(gating, 1)
            held.append(dense_open(b, s_ring))
        run(gating)
        allowed_weights(to_ring)
        held.append(dense_open(B - 1, s_ring))
        for h in range(2):
            weighted(h, to_ring)
        for b in range(B):
            lora(b, y_ring, held[b - HB] if b >= HB else None)
        nc.sync.wait_ge(s_out, 16 * B)


def constants():
    import numpy as np

    c = np.zeros((P, CONST), np.float32)
    c[:, C_ID:C_ID + P] = np.eye(P)
    for p in range(P):
        c[p, C_MASK + (p // HD0) % G0] = 1.0
    c[:, C_IOTA:C_IOTA + 16] = np.arange(16)
    c[:, C_EPS] = LN_EPS
    return c


def selectors():
    import numpy as np

    s = np.zeros((P, KT, P), np.float32)
    for m in range(KT):
        for col in range(P):
            j, d = col // (G0 * HD0), col % HD0
            s[(2 * m + j) * HD0 + d, m, col] = 1.0
    return s


def layout(i):
    import numpy as np

    def rows(w):
        return w.reshape(w.shape[0] // P, P, w.shape[1]).transpose(1, 0, 2)

    def row(v):
        return v.reshape(1, -1)

    a = {k: np.asarray(v) for k, v in i.items()}
    wffn = np.stack([
        np.stack([rows(w.T).reshape(P, 2, 512) for w in (g, u, d)], axis=1)
        for g, u, d in [(a["L0_ffn_Sg"], a["L0_ffn_Su"], a["L0_ffn_Sd"]),
                        *zip(a["L0_ffn_Wg"], a["L0_ffn_Wu"], a["L0_ffn_Wd"])]])
    by_head = lambda w: rows(w).reshape(P, KT, w.shape[1] // P, P).transpose(2, 0, 1, 3).reshape(-1, P, D)
    lora_a = a["L1_ffn_lora_A"].transpose(1, 0, 2).reshape(D, E1 * R1)
    laid = {
        "consts": constants(),
        "sel": selectors(),
        "x": a["x"],
        "ctxT": rows(a["ctx_4096"].reshape(B * P, D).T).reshape(P, KT, 2, HT).transpose(2, 0, 1, 3),
        "wq0": rows(a["L0_xattn_Wq"]),
        "wkv0": np.stack([rows(a["L0_xattn_Wk"]), rows(a["L0_xattn_Wv"])], axis=1),
        "wo0": a["L0_xattn_Wo"].reshape(KV0, G0, HD0, D).transpose(0, 2, 1, 3).reshape(P, G0, D),
        "bq0": a["L0_xattn_bq"].reshape(KT, P).T,
        "bk0": a["L0_xattn_bk"].reshape(P, 1),
        "bv0": row(a["L0_xattn_bv"]),
        "bo0": row(a["L0_xattn_bo"]),
        "gate0": rows(a["L0_ffn_gate_w"].T),
        "gbias0": row(a["L0_ffn_bias"]),
        "wffn": wffn,
        "wk1": by_head(a["L1_xattn_Wk"]),
        "wv1": a["L1_xattn_Wv"].reshape(KT, P, D),
        "wq1": by_head(a["L1_xattn_Wq"]),
        "wo1": a["L1_xattn_Wo"].reshape(H1, P, D),
        "wm1": rows(a["L1_ffn_weight"].T),
        "ws1": rows(np.concatenate([lora_a, a["L1_ffn_gw1"].T], axis=1)),
        "lb1": a["L1_ffn_lora_B"].reshape(E1 * R1, D),
        "gb1": a["L1_ffn_gb1"].reshape(G1, 1),
        "vecs1": row(np.concatenate([a["L1_ffn_ln_gamma"], a["L1_ffn_ln_beta"], a["L1_ffn_gb2"]])),
        "gw2": a["L1_ffn_gw2"].reshape(1, E1, G1),
    }
    return {k: np.ascontiguousarray(v) for k, v in laid.items()}


def kernel(**inputs):
    import concourse.bacc as bacc
    from concourse.bass_utils import run_bass_kernel_spmd

    laid = layout(inputs)
    nc = bacc.Bacc("TRN2", target_bir_lowering=False, num_devices=1)
    A = {name: nc.dram_tensor("in_" + name, a.shape, mybir.dt.from_np(a.dtype), kind="ExternalInput").ap()
         for name, a in laid.items()}
    out = nc.dram_tensor("out", (B, P, D), F32, kind="ExternalOutput").ap()
    layers_kernel(nc, A, out)
    r = run_bass_kernel_spmd(nc, [{"in_" + name: a for name, a in laid.items()}], core_ids=[0])
    return r.results[0]["out"]
```
